# Optimizing a Trainium2 kernel written in Bass

```python
import numpy as np
import jax
import jax.numpy as jnp

def _softmax(x, axis=-1):
    return jax.nn.softmax(x, axis=axis)

def _gelu(x):
    return jax.nn.gelu(x, approximate=True)

def _silu(x):
    return jax.nn.silu(x)

def _sigmoid(x):
    return jax.nn.sigmoid(x)

def _layernorm(x, axis=-1, eps=1e-05):
    m = jnp.mean(x, axis=axis, keepdims=True)
    v = jnp.var(x, axis=axis, keepdims=True)
    return (x - m) / jnp.sqrt(v + eps)

def _scatter_add(tgt, idx, src, axis=0):
    return tgt.at[idx].add(src)

def _segment_sum(src, seg, n):
    return jax.ops.segment_sum(src, seg, n)
kernel_name = 'mk_prb_d2_jaxref_r8_458960'

def setup_inputs(seed: int=0):
    np.random.seed(seed)
    _w = jnp.asarray

    def _L0_attn_setup():
        import jax, jax.numpy as jnp
        import numpy as np
        H, NS = (16, 8)
        key = jax.random.key(seed)
        ks = jax.random.split(key, 8)
        B, S, Dm = (1, 256, 256)
        hd = Dm // H
        return {'hidden_states': jax.random.normal(ks[0], (B, S, Dm), jnp.float32), 'Wq': jax.random.normal(ks[1], (Dm, Dm), jnp.float32) * 0.02, 'Wk': jax.random.normal(ks[2], (Dm, Dm), jnp.float32) * 0.02, 'Wv': jax.random.normal(ks[3], (Dm, Dm), jnp.float32) * 0.02, 'Wo': jax.random.normal(ks[4], (Dm, Dm), jnp.float32) * 0.02, 'splat_positions': jax.random.normal(ks[5], (H, NS, hd), jnp.float32) * 0.02, 'splat_directions': jax.random.normal(ks[6], (H, NS, hd), jnp.float32) * 0.02, 'splat_log_scales': jnp.full((H, NS), np.float32(np.log(0.8)), jnp.float32), 'splat_log_amplitudes': jnp.full((H, NS), np.float32(-np.log(NS)), jnp.float32), 'directional_strength': jnp.float32(0.4), 'position_sensitivity': jnp.float32(0.3), 'gsa_strength': jnp.float32(-4.0)}
    _L0_attn_in = _L0_attn_setup()

    def _L0_ffn_setup():
        import jax, jax.numpy as jnp
        import numpy as np
        B, S, H, I = (1, 64, 256, 768)

        def _quantized_matmul(x, w, scale):
            wq = w.astype(jnp.float8_e4m3fn).astype(x.dtype)
            y = jnp.einsum('bsi,io->bso', x, wq)
            return y * scale
        key = jax.random.key(seed)
        ks = jax.random.split(key, 7)
        return {'x': jax.random.normal(ks[0], (B, S, H), dtype=jnp.float32), 'gate_w': jax.random.normal(ks[1], (H, I), dtype=jnp.float32) * 0.02, 'up_w': jax.random.normal(ks[2], (H, I), dtype=jnp.float32) * 0.02, 'down_w': jax.random.normal(ks[3], (I, H), dtype=jnp.float32) * 0.02, 'gate_scale': jax.random.uniform(ks[4], (I,), dtype=jnp.float32, minval=0.5, maxval=1.5), 'up_scale': jax.random.uniform(ks[5], (I,), dtype=jnp.float32, minval=0.5, maxval=1.5), 'down_scale': jax.random.uniform(ks[6], (H,), dtype=jnp.float32, minval=0.5, maxval=1.5)}
    _L0_ffn_in = _L0_ffn_setup()

    def _L1_attn_setup():
        import jax, jax.numpy as jnp
        import numpy as np
        NUM_STEPS = 3
        NUM_HEADS = 8
        HEAD_DIM = 128
        EPS = 1e-05

        def layernorm(x, g, b):
            mu = jnp.mean(x, -1, keepdims=True)
            var = jnp.mean(jnp.square(x - mu), -1, keepdims=True)
            return (x - mu) * jax.lax.rsqrt(var + EPS) * g + b

        def entmax15(x):
            x = (x - jnp.max(x, -1, keepdims=True)) / 2.0
            xs = jnp.flip(jnp.sort(x, -1), -1)
            rho = jnp.arange(1, x.shape[-1] + 1, dtype=x.dtype)
            mean = jnp.cumsum(xs, -1) / rho
            meansq = jnp.cumsum(xs * xs, -1) / rho
            ss = rho * (meansq - jnp.square(mean))
            tau = mean - jnp.sqrt(jnp.clip((1.0 - ss) / rho, 0.0, None))
            support = jnp.sum(tau <= xs, -1, keepdims=True)
            tau_star = jnp.take_along_axis(tau, support - 1, -1)
            return jnp.square(jnp.clip(x - tau_star, 0.0, None))
        key = jax.random.key(seed)
        ks = jax.random.split(key, 6)
        B, S, Hd, Md, N = (2, 128, 256, 128, 256)
        THD = NUM_HEADS * HEAD_DIM
        return {'hidden': jax.random.normal(ks[0], (B, S, Hd), jnp.float32), 'memory': jax.random.normal(ks[1], (N, Md), jnp.float32), 'Wq': jax.random.normal(ks[2], (THD, Hd), jnp.float32) / np.float32(np.sqrt(Hd)), 'Wk': jax.random.normal(ks[3], (THD, Md), jnp.float32) / np.float32(np.sqrt(Md)), 'Wv': jax.random.normal(ks[4], (THD, Md), jnp.float32) / np.float32(np.sqrt(Md)), 'Wo': jax.random.normal(ks[5], (Hd, THD), jnp.float32) / np.float32(np.sqrt(THD)), 'log_beta': jnp.full((NUM_HEADS,), float(np.log(1.0 / np.sqrt(HEAD_DIM))), jnp.float32), 'g_state': jnp.ones((Hd,), jnp.float32), 'b_state': jnp.zeros((Hd,), jnp.float32), 'g_mem': jnp.ones((Md,), jnp.float32), 'b_mem': jnp.zeros((Md,), jnp.float32)}
    _L1_attn_in = _L1_attn_setup()

    def _L1_ffn_setup():
        import jax, jax.numpy as jnp
        import numpy as np
        B, S, H = (4, 128, 256)
        NH = 16
        HD = H // NH
        RD = HD // 2
        LAT = H // 4
        I = 128
        NE = 8
        NSH = 1
        NR = NE - NSH
        TOPK = 2
        EPS = 1e-05
        SCALING = 8.0

        def _w(key, shape, fan_in):
            return jax.random.normal(key, shape, dtype=jnp.float32) / np.sqrt(fan_in)

        def rmsnorm(x, w):
            rms = jax.lax.rsqrt(jnp.mean(x * x, axis=-1, keepdims=True) + EPS)
            return w * rms * x

        def rope_cos_sin(seq_len):
            inv_freq = 1.0 / 10000.0 ** (jnp.arange(0, RD, 2, dtype=jnp.float32) / RD)
            t = jnp.arange(seq_len, dtype=jnp.float32)
            ang = jnp.outer(t, inv_freq)
            emb = jnp.concatenate([ang, ang], axis=-1)
            return (jnp.cos(emb), jnp.sin(emb))

        def apply_rope(x, cos, sin):
            c = cos[None, :, None, :]
            s = sin[None, :, None, :]
            x1, x2 = jnp.split(x, 2, axis=-1)
            rot = jnp.concatenate([-x2, x1], axis=-1)
            return x * c + rot * s

        def expert_ffn(x, wg, wu, wd):
            h = jax.nn.silu(x @ wg) * (x @ wu) / SCALING
            return h @ wd

        def attention(x, kv_d_w, q_d_w, k_u_w, v_u_w, q_u_w, rope_k_w, rope_q_w, o_w):
            b, s, _ = x.shape
            kv_d = x @ kv_d_w
            q_d = x @ q_d_w
            k_p = (kv_d @ k_u_w).reshape(b, s, NH, RD)
            q_p = (q_d @ q_u_w).reshape(b, s, NH, RD)
            v = (kv_d @ v_u_w).reshape(b, s, NH, HD)
            k_r = (x @ rope_k_w).reshape(b, s, NH, RD)
            q_r = (q_d @ rope_q_w).reshape(b, s, NH, RD)
            cos, sin = rope_cos_sin(s)
            k_r = apply_rope(k_r, cos, sin)
            q_r = apply_rope(q_r, cos, sin)
            k = jnp.concatenate([k_p, k_r], axis=-1)
            q = jnp.concatenate([q_p, q_r], axis=-1)
            scale = 1.0 / np.sqrt(HD)
            scores = jnp.einsum('bqhd,bkhd->bhqk', q, k) * scale
            causal = jnp.tril(jnp.ones((s, s), dtype=bool))
            scores = jnp.where(causal[None, None], scores, jnp.finfo(scores.dtype).min)
            probs = jax.nn.softmax(scores, axis=-1)
            out = jnp.einsum('bhqk,bkhd->bqhd', probs, v).reshape(b, s, H)
            return out @ o_w

        def moe(x, sh_gate, sh_up, sh_down, r_gate, r_up, r_down, router_w, router_b):
            shared = expert_ffn(x, sh_gate, sh_up, sh_down)
            logits = x @ router_w + router_b
            probs = jax.nn.sigmoid(logits)
            scores, idx = jax.lax.top_k(probs, TOPK)
            scores = scores / jnp.sum(scores, axis=-1, keepdims=True)
            w = jnp.sum(jax.nn.one_hot(idx, NR, dtype=x.dtype) * scores[..., None], axis=-2)
            combined = jnp.zeros_like(x)
            for e in range(NR):
                combined = combined + w[..., e:e + 1] * expert_ffn(x, r_gate[e], r_up[e], r_down[e])
            return shared + combined
        key = jax.random.key(seed)
        ks = jax.random.split(key, 24)
        return {'x': jax.random.normal(ks[0], (B, S, H), dtype=jnp.float32), 'ln1_w': jnp.ones((H,), jnp.float32), 'ln2_w': jnp.ones((H,), jnp.float32), 'kv_d_w': _w(ks[1], (H, LAT), H), 'q_d_w': _w(ks[2], (H, LAT), H), 'k_u_w': _w(ks[3], (LAT, H // 2), LAT), 'v_u_w': _w(ks[4], (LAT, H), LAT), 'q_u_w': _w(ks[5], (LAT, H // 2), LAT), 'rope_k_w': _w(ks[6], (H, H // 2), H), 'rope_q_w': _w(ks[7], (LAT, H // 2), LAT), 'o_w': _w(ks[8], (H, H), H), 'sh_gate': _w(ks[9], (H, I), H), 'sh_up': _w(ks[10], (H, I), H), 'sh_down': _w(ks[11], (I, H), I), 'r_gate': _w(ks[12], (NR, H, I), H), 'r_up': _w(ks[13], (NR, H, I), H), 'r_down': _w(ks[14], (NR, I, H), I), 'router_w': _w(ks[15], (H, NR), H), 'router_b': jnp.zeros((NR,), jnp.float32)}
    _L1_ffn_in = _L1_ffn_setup()
    _d = {'L0_attn_hidden_states': _L0_attn_in['hidden_states'], 'L0_attn_Wq': _L0_attn_in['Wq'], 'L0_attn_Wk': _L0_attn_in['Wk'], 'L0_attn_Wv': _L0_attn_in['Wv'], 'L0_attn_Wo': _L0_attn_in['Wo'], 'L0_attn_splat_positions': _L0_attn_in['splat_positions'], 'L0_attn_splat_directions': _L0_attn_in['splat_directions'], 'L0_attn_splat_log_scales': _L0_attn_in['splat_log_scales'], 'L0_attn_splat_log_amplitudes': _L0_attn_in['splat_log_amplitudes'], 'L0_attn_directional_strength': _L0_attn_in['directional_strength'], 'L0_attn_position_sensitivity': _L0_attn_in['position_sensitivity'], 'L0_attn_gsa_strength': _L0_attn_in['gsa_strength'], 'L0_ffn_gate_w': _L0_ffn_in['gate_w'], 'L0_ffn_up_w': _L0_ffn_in['up_w'], 'L0_ffn_down_w': _L0_ffn_in['down_w'], 'L0_ffn_gate_scale': _L0_ffn_in['gate_scale'], 'L0_ffn_up_scale': _L0_ffn_in['up_scale'], 'L0_ffn_down_scale': _L0_ffn_in['down_scale'], 'L1_attn_memory': _L1_attn_in['memory'], 'L1_attn_Wq': _L1_attn_in['Wq'], 'L1_attn_Wk': _L1_attn_in['Wk'], 'L1_attn_Wv': _L1_attn_in['Wv'], 'L1_attn_Wo': _L1_attn_in['Wo'], 'L1_attn_log_beta': _L1_attn_in['log_beta'], 'L1_attn_g_state': _L1_attn_in['g_state'], 'L1_attn_b_state': _L1_attn_in['b_state'], 'L1_attn_g_mem': _L1_attn_in['g_mem'], 'L1_attn_b_mem': _L1_attn_in['b_mem'], 'L1_ffn_ln1_w': _L1_ffn_in['ln1_w'], 'L1_ffn_ln2_w': _L1_ffn_in['ln2_w'], 'L1_ffn_kv_d_w': _L1_ffn_in['kv_d_w'], 'L1_ffn_q_d_w': _L1_ffn_in['q_d_w'], 'L1_ffn_k_u_w': _L1_ffn_in['k_u_w'], 'L1_ffn_v_u_w': _L1_ffn_in['v_u_w'], 'L1_ffn_q_u_w': _L1_ffn_in['q_u_w'], 'L1_ffn_rope_k_w': _L1_ffn_in['rope_k_w'], 'L1_ffn_rope_q_w': _L1_ffn_in['rope_q_w'], 'L1_ffn_o_w': _L1_ffn_in['o_w'], 'L1_ffn_sh_gate': _L1_ffn_in['sh_gate'], 'L1_ffn_sh_up': _L1_ffn_in['sh_up'], 'L1_ffn_sh_down': _L1_ffn_in['sh_down'], 'L1_ffn_r_gate': _L1_ffn_in['r_gate'], 'L1_ffn_r_up': _L1_ffn_in['r_up'], 'L1_ffn_r_down': _L1_ffn_in['r_down'], 'L1_ffn_router_w': _L1_ffn_in['router_w'], 'L1_ffn_router_b': _L1_ffn_in['router_b']}
    _x0 = _d['L0_attn_hidden_states']
    _d['L0_attn_hidden_states'] = jax.random.normal(jax.random.fold_in(jax.random.key(seed), 1), (2, 1024, 256), dtype=_x0.dtype)
    del _x0
    return _d

def reference(L0_attn_hidden_states, L0_attn_Wq, L0_attn_Wk, L0_attn_Wv, L0_attn_Wo, L0_attn_splat_positions, L0_attn_splat_directions, L0_attn_splat_log_scales, L0_attn_splat_log_amplitudes, L0_attn_directional_strength, L0_attn_position_sensitivity, L0_attn_gsa_strength, L0_ffn_gate_w, L0_ffn_up_w, L0_ffn_down_w, L0_ffn_gate_scale, L0_ffn_up_scale, L0_ffn_down_scale, L1_attn_memory, L1_attn_Wq, L1_attn_Wk, L1_attn_Wv, L1_attn_Wo, L1_attn_log_beta, L1_attn_g_state, L1_attn_b_state, L1_attn_g_mem, L1_attn_b_mem, L1_ffn_ln1_w, L1_ffn_ln2_w, L1_ffn_kv_d_w, L1_ffn_q_d_w, L1_ffn_k_u_w, L1_ffn_v_u_w, L1_ffn_q_u_w, L1_ffn_rope_k_w, L1_ffn_rope_q_w, L1_ffn_o_w, L1_ffn_sh_gate, L1_ffn_sh_up, L1_ffn_sh_down, L1_ffn_r_gate, L1_ffn_r_up, L1_ffn_r_down, L1_ffn_router_w, L1_ffn_router_b):

    def _L0_attn_ref(hidden_states, Wq, Wk, Wv, Wo, splat_positions, splat_directions, splat_log_scales, splat_log_amplitudes, directional_strength, position_sensitivity, gsa_strength):
        import jax, jax.numpy as jnp
        import numpy as np
        H, NS = (16, 8)
        B, S, Dm = hidden_states.shape
        Hn, Ns, hd = splat_positions.shape

        def heads(x):
            return x.reshape(B, S, Hn, hd).transpose(0, 2, 1, 3)
        q = heads(hidden_states @ Wq.T)
        k = heads(hidden_states @ Wk.T)
        v = heads(hidden_states @ Wv.T)
        scores = jnp.einsum('bhid,bhjd->bhij', q, k) / jnp.sqrt(jnp.float32(hd))
        mask = jnp.tril(jnp.ones((S, S), bool))
        neg = jnp.finfo(scores.dtype).min

        def out_proj(attn):
            o = jnp.einsum('bhij,bhjd->bhid', attn, v)
            return o.transpose(0, 2, 1, 3).reshape(B, S, Dm) @ Wo.T
        std_out = out_proj(jax.nn.softmax(jnp.where(mask, scores, neg), axis=-1))
        scales = jnp.exp(splat_log_scales)
        amps = jnp.exp(splat_log_amplitudes)
        dirn = splat_directions / (jnp.linalg.norm(splat_directions, axis=-1, keepdims=True) + 1e-08)

        def splat_feats(x):
            diff = x[:, :, :, None, :] - splat_positions[None, :, None, :, :]
            gauss = jnp.exp(-0.5 * jnp.sum(diff * diff, -1) / (scales ** 2)[None, :, None, :])
            dirp = jnp.tanh(jnp.einsum('bhsnd,hnd->bhsn', diff, dirn))
            return (gauss, dirp)
        qg, qd = splat_feats(q)
        kg, kd = splat_feats(k)
        amp_b = amps[None, :, None, :]
        splat_attn = jnp.einsum('bhin,bhjn->bhij', amp_b * qg, kg) + directional_strength * jnp.einsum('bhin,bhjn->bhij', amp_b * qg * qd, kg * kd)
        gsa_scores = scores + position_sensitivity * splat_attn
        gsa_out = out_proj(jax.nn.softmax(jnp.where(mask, gsa_scores, neg), axis=-1))
        blend = jnp.minimum(jnp.float32(0.03), jax.nn.sigmoid(gsa_strength) * 0.15)
        return (1.0 - blend) * std_out + blend * gsa_out

    def _L0_ffn_ref(x, gate_w, up_w, down_w, gate_scale, up_scale, down_scale):
        import jax, jax.numpy as jnp
        import numpy as np
        B, S, H, I = (1, 64, 256, 768)

        def _quantized_matmul(x, w, scale):
            wq = w.astype(jnp.float8_e4m3fn).astype(x.dtype)
            y = jnp.einsum('bsi,io->bso', x, wq)
            return y * scale
        gate = jax.nn.silu(_quantized_matmul(x, gate_w, gate_scale))
        up = _quantized_matmul(x, up_w, up_scale)
        fuse = gate * up
        return _quantized_matmul(fuse, down_w, down_scale)

    def _L1_attn_ref(hidden, memory, Wq, Wk, Wv, Wo, log_beta, g_state, b_state, g_mem, b_mem):
        import jax, jax.numpy as jnp
        import numpy as np
        NUM_STEPS = 3
        NUM_HEADS = 8
        HEAD_DIM = 128
        EPS = 1e-05

        def layernorm(x, g, b):
            mu = jnp.mean(x, -1, keepdims=True)
            var = jnp.mean(jnp.square(x - mu), -1, keepdims=True)
            return (x - mu) * jax.lax.rsqrt(var + EPS) * g + b

        def entmax15(x):
            x = (x - jnp.max(x, -1, keepdims=True)) / 2.0
            xs = jnp.flip(jnp.sort(x, -1), -1)
            rho = jnp.arange(1, x.shape[-1] + 1, dtype=x.dtype)
            mean = jnp.cumsum(xs, -1) / rho
            meansq = jnp.cumsum(xs * xs, -1) / rho
            ss = rho * (meansq - jnp.square(mean))
            tau = mean - jnp.sqrt(jnp.clip((1.0 - ss) / rho, 0.0, None))
            support = jnp.sum(tau <= xs, -1, keepdims=True)
            tau_star = jnp.take_along_axis(tau, support - 1, -1)
            return jnp.square(jnp.clip(x - tau_star, 0.0, None))
        B, S, _ = hidden.shape
        N = memory.shape[0]
        H, hd = (NUM_HEADS, HEAD_DIM)
        Q = layernorm(hidden, g_state, b_state) @ Wq.T
        mn = layernorm(memory, g_mem, b_mem)
        K = (mn @ Wk.T).reshape(N, H, hd).transpose(1, 0, 2)
        V = (mn @ Wv.T).reshape(N, H, hd).transpose(1, 0, 2)
        xi = Q.reshape(B, S, H, hd).transpose(0, 2, 1, 3)
        beta = jnp.exp(log_beta)[None, :, None, None]
        for _ in range(NUM_STEPS):
            scores = jnp.einsum('bhsd,hnd->bhsn', xi, K) * beta
            w = entmax15(scores)
            xi = jnp.einsum('bhsn,hnd->bhsd', w, V)
        out = xi.transpose(0, 2, 1, 3).reshape(B, S, H * hd) @ Wo.T
        return out

    def _L1_ffn_ref(x, ln1_w, ln2_w, kv_d_w, q_d_w, k_u_w, v_u_w, q_u_w, rope_k_w, rope_q_w, o_w, sh_gate, sh_up, sh_down, r_gate, r_up, r_down, router_w, router_b):
        import jax, jax.numpy as jnp
        import numpy as np
        B, S, H = (4, 128, 256)
        NH = 16
        HD = H // NH
        RD = HD // 2
        LAT = H // 4
        I = 128
        NE = 8
        NSH = 1
        NR = NE - NSH
        TOPK = 2
        EPS = 1e-05
        SCALING = 8.0

        def _w(key, shape, fan_in):
            return jax.random.normal(key, shape, dtype=jnp.float32) / np.sqrt(fan_in)

        def rmsnorm(x, w):
            rms = jax.lax.rsqrt(jnp.mean(x * x, axis=-1, keepdims=True) + EPS)
            return w * rms * x

        def rope_cos_sin(seq_len):
            inv_freq = 1.0 / 10000.0 ** (jnp.arange(0, RD, 2, dtype=jnp.float32) / RD)
            t = jnp.arange(seq_len, dtype=jnp.float32)
            ang = jnp.outer(t, inv_freq)
            emb = jnp.concatenate([ang, ang], axis=-1)
            return (jnp.cos(emb), jnp.sin(emb))

        def apply_rope(x, cos, sin):
            c = cos[None, :, None, :]
            s = sin[None, :, None, :]
            x1, x2 = jnp.split(x, 2, axis=-1)
            rot = jnp.concatenate([-x2, x1], axis=-1)
            return x * c + rot * s

        def expert_ffn(x, wg, wu, wd):
            h = jax.nn.silu(x @ wg) * (x @ wu) / SCALING
            return h @ wd

        def attention(x, kv_d_w, q_d_w, k_u_w, v_u_w, q_u_w, rope_k_w, rope_q_w, o_w):
            b, s, _ = x.shape
            kv_d = x @ kv_d_w
            q_d = x @ q_d_w
            k_p = (kv_d @ k_u_w).reshape(b, s, NH, RD)
            q_p = (q_d @ q_u_w).reshape(b, s, NH, RD)
            v = (kv_d @ v_u_w).reshape(b, s, NH, HD)
            k_r = (x @ rope_k_w).reshape(b, s, NH, RD)
            q_r = (q_d @ rope_q_w).reshape(b, s, NH, RD)
            cos, sin = rope_cos_sin(s)
            k_r = apply_rope(k_r, cos, sin)
            q_r = apply_rope(q_r, cos, sin)
            k = jnp.concatenate([k_p, k_r], axis=-1)
            q = jnp.concatenate([q_p, q_r], axis=-1)
            scale = 1.0 / np.sqrt(HD)
            scores = jnp.einsum('bqhd,bkhd->bhqk', q, k) * scale
            causal = jnp.tril(jnp.ones((s, s), dtype=bool))
            scores = jnp.where(causal[None, None], scores, jnp.finfo(scores.dtype).min)
            probs = jax.nn.softmax(scores, axis=-1)
            out = jnp.einsum('bhqk,bkhd->bqhd', probs, v).reshape(b, s, H)
            return out @ o_w

        def moe(x, sh_gate, sh_up, sh_down, r_gate, r_up, r_down, router_w, router_b):
            shared = expert_ffn(x, sh_gate, sh_up, sh_down)
            logits = x @ router_w + router_b
            probs = jax.nn.sigmoid(logits)
            scores, idx = jax.lax.top_k(probs, TOPK)
            scores = scores / jnp.sum(scores, axis=-1, keepdims=True)
            w = jnp.sum(jax.nn.one_hot(idx, NR, dtype=x.dtype) * scores[..., None], axis=-2)
            combined = jnp.zeros_like(x)
            for e in range(NR):
                combined = combined + w[..., e:e + 1] * expert_ffn(x, r_gate[e], r_up[e], r_down[e])
            return shared + combined
        h = x + attention(rmsnorm(x, ln1_w), kv_d_w, q_d_w, k_u_w, v_u_w, q_u_w, rope_k_w, rope_q_w, o_w)
        out = h + moe(rmsnorm(h, ln2_w), sh_gate, sh_up, sh_down, r_gate, r_up, r_down, router_w, router_b)
        return out
    x = L0_attn_hidden_states
    xn = _layernorm(x, axis=-1)
    x = x + _L0_attn_ref(xn, L0_attn_Wq, L0_attn_Wk, L0_attn_Wv, L0_attn_Wo, L0_attn_splat_positions, L0_attn_splat_directions, L0_attn_splat_log_scales, L0_attn_splat_log_amplitudes, L0_attn_directional_strength, L0_attn_position_sensitivity, L0_attn_gsa_strength) + _L0_ffn_ref(xn, L0_ffn_gate_w, L0_ffn_up_w, L0_ffn_down_w, L0_ffn_gate_scale, L0_ffn_up_scale, L0_ffn_down_scale)
    xn = _layernorm(x, axis=-1)
    x = x + _L1_attn_ref(xn, L1_attn_memory, L1_attn_Wq, L1_attn_Wk, L1_attn_Wv, L1_attn_Wo, L1_attn_log_beta, L1_attn_g_state, L1_attn_b_state, L1_attn_g_mem, L1_attn_b_mem) + _L1_ffn_ref(xn, L1_ffn_ln1_w, L1_ffn_ln2_w, L1_ffn_kv_d_w, L1_ffn_q_d_w, L1_ffn_k_u_w, L1_ffn_v_u_w, L1_ffn_q_u_w, L1_ffn_rope_k_w, L1_ffn_rope_q_w, L1_ffn_o_w, L1_ffn_sh_gate, L1_ffn_sh_up, L1_ffn_sh_down, L1_ffn_r_gate, L1_ffn_r_up, L1_ffn_r_down, L1_ffn_router_w, L1_ffn_router_b)
    return x

_drawn_inputs = setup_inputs


def setup_inputs(seed=0):
    import zlib

    import numpy as np

    out = dict(_drawn_inputs(seed))
    spreads = {'L0_attn_splat_log_scales': (-0.2231435477733612, 0.6),
     'L0_attn_splat_log_amplitudes': (-2.079441547393799, 0.6),
     'L1_attn_log_beta': (-2.4260151386260986, 0.2),
     'L1_attn_g_state': (1.0, 0.2),
     'L1_attn_b_state': (0.0, 0.279),
     'L1_attn_g_mem': (1.0, 0.2),
     'L1_attn_b_mem': (0.0, 0.1),
     'L1_ffn_ln1_w': (1.0, 0.553),
     'L1_ffn_ln2_w': (1.0, 0.6),
     'L1_ffn_router_b': (0.0, 2.0)}
    factors = {'L0_attn_Wq': 8.0,
     'L0_attn_Wk': 8.0,
     'L0_attn_Wv': 4.466,
     'L0_attn_Wo': 4.456,
     'L0_attn_splat_positions': 8.0,
     'L0_attn_splat_directions': 8.0,
     'L0_ffn_gate_scale': 4.036,
     'L0_ffn_up_scale': 4.66,
     'L0_ffn_down_scale': 4.518,
     'L1_ffn_r_gate': 2.771,
     'L1_ffn_router_w': 3.16}
    for name, (base, spread) in spreads.items():
        noise = np.random.default_rng([zlib.crc32(name.encode()), seed]).standard_normal(out[name].shape)
        drawn = base * np.exp(spread * noise) if base else spread * noise
        out[name] = jnp.asarray(drawn.astype(out[name].dtype))
    for name, factor in factors.items():
        out[name] = (out[name] * factor).astype(out[name].dtype)
    return out
```

```python
from contextlib import ExitStack, contextmanager

import numpy as np
import concourse.bass as bass
from concourse import mybir

F32 = mybir.dt.float32
F32R = mybir.dt.float32r
BF16 = mybir.dt.bfloat16
U32 = mybir.dt.uint32
ALU = mybir.AluOpType
ACT = mybir.ActivationFunctionType
X_AXIS = mybir.AxisListType.X
FUNCTION = type(lambda: 0)
ds = bass.ds

START = 2048


class Counter:

    def __init__(self, sem, step):
        self.sem, self.step, self.per_stage = sem, step, {}


class Program:

    def __init__(self):
        self.stages, self.lines, self.counters, self.marks = [], [], [], {}
        self.stage()

    def stage(self, trips=1):
        self.stages.append(trips)
        self.now = len(self.stages) - 1
        self.marks = {}
        self.pending = []

    def loop(self, trips):
        self.barrier()
        self.stage(trips)

    def end_loop(self):
        self.stage()
        self.barrier()

    def barrier(self):
        if self.stages[self.now] != 1:
            raise ValueError("no barrier inside a loop")
        now = self.now
        at = [(c, c.per_stage.get(now, 0)) for c in self.counters]
        for line in self.lines:
            for c, local in at:
                line.queue.append((now, {"at": (c, local), "lag": 0}))

    def mark(self, name, where):
        self.marks[name] = where
        for waited, found in self.pending:
            if waited == name:
                found["at"] = where

    def alias(self, name, other):
        self.mark(name, self.marks[other])

    def value(self, counter, local, now, lag):
        base = START + sum(self.stages[s] * counter.per_stage.get(s, 0) for s in range(now))
        return base + local - lag * counter.per_stage.get(now, 0)


class Line:

    def __init__(self, program, sem):
        self.program, self.counter, self.queue = program, Counter(sem, 1), []
        program.lines.append(self)
        program.counters.append(self.counter)

    def wait(self, *names):
        program = self.program
        for name in names:
            if name in program.marks:
                counter, local = program.marks[name]
                self.queue.append((program.now, {"at": (counter, local), "lag": 0}))
            elif program.stages[program.now] != 1:
                found = {"lag": 1}
                program.pending.append((name, found))
                self.queue.append((program.now, found))

    def op(self, emit, name=None, counter=None):
        program = self.program
        if name is None and counter is None:
            self.queue.append((program.now, emit))
            return
        c = counter or self.counter
        c.per_stage[program.now] = c.per_stage.get(program.now, 0) + c.step
        self.queue.append((program.now, lambda engine, i: emit(engine, i).then_inc(c.sem, c.step)))
        if name is not None:
            program.mark(name, (c, c.per_stage[program.now]))

    def starts(self):
        return [self.counter]

    def play(self, engine):
        program = self.program
        assert all(n <= START for c in program.counters for n in c.per_stage.values())
        for counter in self.starts():
            engine.sem_inc(counter.sem, START)
        for s, trips in enumerate(program.stages):
            body = [entry for stage, entry in self.queue if stage == s]
            if body and trips == 1:
                self.play_body(engine, body, s, 0)
            elif body:
                with engine.Fori(0, trips) as i:
                    self.play_body(engine, body, s, i)

    def play_body(self, engine, body, now, i):
        program, wanted, reached = self.program, {}, {}
        for entry in body + [None]:
            if type(entry) is dict:
                if "at" in entry:
                    counter, local = entry["at"]
                    value = program.value(counter, local, now, entry["lag"])
                    wanted[counter] = max(value, wanted.get(counter, 0))
                continue
            for counter, value in wanted.items():
                per = 0 if program.stages[now] == 1 else counter.per_stage.get(now, 0)
                if value > reached.get(counter, 0 if per else START):
                    reached[counter] = value
                    engine.wait_ge(counter.sem, i * per + value if per else value)
            wanted = {}
            if entry:
                entry(engine, i)


def at(x, i):
    return x(i) if type(x) is FUNCTION else x


class Tensor(Line):
    def mm(self, out, lhsT, rhs, start=True, stop=True, name=None):
        self.op(lambda e, i: e.matmul(at(out, i), at(lhsT, i), at(rhs, i), start=start, stop=stop), name)

    def transpose(self, out, in_, identity, name=None):
        self.op(lambda e, i: e.transpose(at(out, i), at(in_, i), identity), name)

    def products(self, out, pairs, name=None):
        for n, (lhsT, rhs) in enumerate(pairs):
            last = n == len(pairs) - 1
            self.mm(out, lhsT, rhs, n == 0, last, name if last else None)


class Scalar(Line):
    def act(self, out, in_, func=ACT.Copy, bias=0.0, scale=1.0, accum=None, name=None):
        self.op(lambda e, i: e.activation(at(out, i), at(in_, i), func, bias=at(bias, i), scale=at(scale, i),
                                          accum_out=accum), name)

    def dma(self, out, in_, counter, name):
        self.op(lambda e, i: e.dma_start(at(out, i), at(in_, i)), name, counter)


class Vector(Line):
    def tt(self, out, a, b, op, name=None):
        self.op(lambda e, i: e.tensor_tensor(at(out, i), at(a, i), at(b, i), op), name)

    def ts(self, out, a, s1, op0, s2=None, op1=ALU.bypass, accum=None, name=None):
        self.op(lambda e, i: e.tensor_scalar(at(out, i), at(a, i), at(s1, i), at(s2, i), op0, op1, accum_out=accum), name)

    def stt(self, out, a, s, b, op0, op1, name=None):
        self.op(lambda e, i: e.scalar_tensor_tensor(at(out, i), at(a, i), at(s, i), at(b, i), op0, op1), name)

    def copy(self, out, a, name=None):
        self.op(lambda e, i: e.tensor_copy(at(out, i), at(a, i)), name)

    def recip(self, out, a, name=None):
        self.op(lambda e, i: e.reciprocal(at(out, i), at(a, i)), name)

    def reduce(self, out, a, op, negate=None, name=None):
        self.op(lambda e, i: e.tensor_reduce(at(out, i), at(a, i), X_AXIS, op, negate=negate), name)

    def memset(self, out, v, name=None):
        self.op(lambda e, i: e.memset(out, v), name)


class Sync(Line):
    def starts(self):
        return [self.counter] + [c for c in self.program.counters if c.step == 16]

    def dma(self, out, in_, counter, name):
        self.op(lambda e, i: e.dma_start(at(out, i), at(in_, i)), name, counter)


def f32(x):
    return (lambda i: x(i).bitcast(F32)) if type(x) is FUNCTION else x.bitcast(F32)


P = 128
B, S, D = 2, 1024, 256
T = B * S
NT = T // P
DC = D // P
NB = T // 512
H, HD, NS = 16, 16, 8
QT = S // P
F0 = 768
FC = F0 // P
HH, NM = 8, 256
MC = NM // P
NE, NR = 8, 7
EPS = 1e-5
BIG = -3.0e38
NEWTON = 5

REC = 64
KROW = 96
STACK = KROW + 1


class Kernel:

    def __init__(self, nc, ctx, ins, out):
        self.nc, self.ctx, self.ins, self.out = nc, ctx, ins, out
        self.p = p = Program()
        def sem(n):
            return ctx.enter_context(nc.semaphore(n))
        self.pe, self.act, self.dve = Tensor(p, sem("pe")), Scalar(p, sem("act")), Vector(p, sem("dve"))
        self.pool, self.sp = Vector(p, sem("pool")), Sync(p, sem("sp"))
        self.dma_sems = {}
        self.scopes = [ctx]
        self.n = 0

    def dma_counter(self, name):
        if name not in self.dma_sems:
            c = Counter(self.ctx.enter_context(self.nc.semaphore("dma_" + name)), 16)
            self.p.counters.append(c)
            self.dma_sems[name] = c
        return self.dma_sems[name]

    def sb(self, name, shape, dt=F32):
        self.n += 1
        return self.scopes[-1].enter_context(self.nc.sbuf_tensor(f"{name}_{self.n}", shape, dt))

    def ps(self, name, shape, dt=F32):
        self.n += 1
        n = int(np.prod(shape[1:]))
        t = self.scopes[-1].enter_context(self.nc.psum_tensor(f"{name}_{self.n}", [P, -(-n // 512) * 512], dt))
        dims = "abcd"[:len(shape) - 1]
        return t[:, 0:n].rearrange(f"p ({' '.join(dims)}) -> p {' '.join(dims)}",
                                   **dict(zip(dims, shape[1:]))) if len(dims) > 1 else t[:, 0:n]

    def load(self, *pairs):
        for tile, name in pairs:
            src = self.ins[name]
            self.sp.dma(tile, src, self.dma_counter("weights"), "load_" + name)

    def split(self, hi, lo, src, tag):
        self.act.act(hi, src, name=f"{tag}_hi")
        self.dve.wait(f"{tag}_hi")
        self.dve.tt(lo, src, f32(hi), ALU.subtract, name=f"{tag}_lo")


@contextmanager
def scope(k):
    with ExitStack() as s:
        k.scopes.append(s)
        yield
        k.p.barrier()
        k.scopes.pop()


def constants(k):
    k.ident = k.sb("ident", [P, P])
    k.identb = k.sb("identb", [P, P], BF16)
    k.mask_q = k.sb("mask_q", [P, P], BF16)
    k.mask_k = k.sb("mask_k", [P, P], BF16)
    k.strips = k.sb("strips", [P, 32])
    k.eps = k.sb("eps", [P, 1])
    pool = k.pool
    for n, t in enumerate((k.ident, k.identb, k.mask_q, k.mask_k, k.strips)):
        pool.memset(t[:], 0.0, name="cleared")
    pool.memset(k.eps[:], EPS, name="cleared")
    pool.wait("cleared")

    def diagonal(t, cmp, fill, base, step, mult):
        pool.op(lambda e, i: e.affine_select(out=t, in_=t, compare_op=cmp, fill=fill, base=base,
                                             pattern=[[step, t.shape[1]]], channel_multiplier=mult), "made")
    diagonal(k.ident[:], ALU.not_equal, 1.0, 0, -1, 1)
    diagonal(k.identb[:], ALU.not_equal, 1.0, 0, -1, 1)
    diagonal(k.mask_q[:], ALU.is_ge, BIG, 0, -1, 1)
    diagonal(k.mask_k[:], ALU.is_ge, BIG, 0, 1, -1)
    for c in range(4):
        diagonal(k.strips[:], ALU.not_equal, 1.0, -32 * c, -1, 1)
        pool.wait("made")


def moments(k, x, tag, n=NT, d=D):
    st = k.sb("bn", [P, n, 6])
    mean, var, half = k.sb("mean", [P, n]), k.sb("var", [P, n]), k.sb("half", [P, n])
    v = k.dve
    for t in range(n):
        v.op(lambda e, i, t=t: e.bn_stats(st[:, t, :], x[:, t, :]), "v")
    v.wait("v")
    v.tt(mean[:], st[:, :, 1], st[:, :, 4], ALU.add, name="v")
    v.tt(half[:], st[:, :, 1], st[:, :, 4], ALU.subtract, name="v")
    v.tt(var[:], st[:, :, 2], st[:, :, 5], ALU.add, name="v")
    v.wait("v")
    v.ts(mean[:], mean[:], 0.5, ALU.mult, name="v")
    v.tt(half[:], half[:], half[:], ALU.mult, name="v")
    v.wait("v")
    v.ts(half[:], half[:], 0.25, ALU.mult, name="v")
    v.wait("v")
    v.stt(var[:], var[:], 1.0 / d, half[:], ALU.mult, ALU.add, name="v")
    v.wait("v")
    return mean, var


def inverse_root(k, var, tag):
    k.act.wait("v")
    k.act.act(var[:], var[:], ACT.Sqrt, bias=k.eps[:], name=f"root_{tag}")
    k.dve.wait(f"root_{tag}")
    k.dve.recip(var[:], var[:], name="v")
    k.dve.wait("v")
    return var


def first_norm(k):
    vals = k.vals
    with scope(k):
        wv, wvh, wvl = k.sb("wv", [P, DC, D]), k.sb("wvh", [P, DC, D], F32R), k.sb("wvl", [P, DC, D], F32R)
        k.load((k.x[:, 0:NT // 2], "x_a"), (k.x[:, NT // 2:], "x_b"), (wv[:], "wv0"))
        k.p.barrier()
        k.split(wvh[:], wvl[:], wv[:], "wv")
        mean, var = moments(k, k.x, "ln0")
        inverse_root(k, var, "ln0")
        k.pool.memset(vals[:], 0.0, name="vals0")
        k.pool.wait("vals0")
        k.pool.memset(vals[:, :, :, HD:HD + 1], 1.0, name="vals1")
        xn = [k.sb("xn", [P, D]) for _ in range(2)]
        th = [k.sb("th", [P, DC, P], F32R) for _ in range(2)]
        tl = [k.sb("tl", [P, DC, P], F32R) for _ in range(2)]
        pt = [k.ps("pt", [P, DC, P]) for _ in range(2)]
        pv = [k.ps("pv", [P, D]) for _ in range(2)]
        k.p.loop(NT // 2)
        for p in range(2):
            def tile(i, p=p):
                return 2 * i + p
            k.dve.wait(f"turned{p}")
            k.dve.ts(xn[p][:], lambda i, p=p: k.x[:, ds(2 * i + p, 1), :],
                     lambda i, p=p: mean[:, ds(2 * i + p, 1)], ALU.subtract,
                     lambda i, p=p: var[:, ds(2 * i + p, 1)], ALU.mult, name=f"xn{p}")
            transposed_tile(k, p, xn, pt, th, tl)
            k.pe.wait(f"v_out{p}", f"th{p}", f"tl{p}")
            k.pe.products(pv[p][:], [(a[:, c, :], w[:, c, :]) for c in range(DC)
                                     for a, w in ((th[p], wvh), (th[p], wvl), (tl[p], wvh))], name=f"v_in{p}")
            k.act.wait(f"v_in{p}")
            k.act.act(lambda i, p=p: vals[:, ds(2 * i + p, 1), :, 0:HD],
                      pv[p][:].rearrange("p (o h d) -> p o h d", o=1, h=H), name=f"v_out{p}")
        k.p.end_loop()


def transposed_tile(k, p, xn, pt, th, tl, scale=None, bias=None):
    xh, xl = k.xh, k.xl
    k.pe.wait(f"xn{p}", f"th{p}", f"tl{p}")
    for c in range(DC):
        k.pe.transpose(pt[p][:, c, :], xn[p][:, c * P:(c + 1) * P], k.ident[:],
                       name=f"turned{p}" if c == DC - 1 else None)
    k.act.wait(f"turned{p}", f"copied{p}", f"v_in{p}")
    k.dve.wait(f"copied{p}", f"v_in{p}")
    if scale is None:
        k.act.act(th[p][:], pt[p][:], name=f"th{p}")
        k.dve.wait(f"th{p}")
        k.dve.tt(tl[p][:], pt[p][:], f32(th[p][:]), ALU.subtract, name=f"tl{p}")
    else:
        for c in range(DC):
            k.act.act(th[p][:, c, :], pt[p][:, c, :], scale=scale[:, c:c + 1], name=f"th{p}")
        k.dve.wait(f"th{p}")
        for c in range(DC):
            k.dve.stt(tl[p][:, c, :], pt[p][:, c, :], scale[:, c:c + 1], f32(th[p][:, c, :]),
                      ALU.mult, ALU.subtract, name=f"tl{p}")
    k.pool.wait(f"th{p}", f"tl{p}")
    k.pool.copy(lambda i, p=p: xh[:, :, ds((2 * i + p) * P, P)], f32(th[p][:]), name=f"copied{p}")
    k.pool.copy(lambda i, p=p: xl[:, :, ds((2 * i + p) * P, P)], f32(tl[p][:]), name=f"copied{p}")


def three(wh, wl, xh, xl, chunks=DC):
    return [(a(c), b(c)) for c in range(chunks) for a, b in ((wh, xh), (wl, xh), (wh, xl))]


def queries_and_keys(k):
    xh, xl = k.xh, k.xl
    with scope(k):
        w, wh, wl = (k.sb(n, [P, DC, 2 * D], t) for n, t in (("w", F32), ("wh", F32R), ("wl", F32R)))
        pos, dirs, half = (k.sb(n, [P, DC, P]) for n in ("pos", "dirs", "half"))
        ph, dh = k.sb("ph", [P, HD]), k.sb("dh", [P, HD])
        sc = k.sb("sc", [P, 5])
        k.load((w[:], "wqk0"), (pos[:], "splat_pos"), (dirs[:], "splat_dir"), (half[:], "neg_half"),
               (ph[:], "pos_rows"), (dh[:], "dir_rows"), (sc[:], "splat_scalars"))
        k.p.barrier()
        k.split(wh[:], wl[:], w[:], "wqk")
        tmp, q = k.sb("tmp", [P, HD]), k.sb("cols", [P, 10])
        inv_s2, b_gauss, inv_n, b_dir, amp = (q[:, n:n + 1] for n in range(5))
        pp, dd, pd = (q[:, n:n + 1] for n in range(5, 8))
        v = k.dve
        k.act.act(inv_s2, sc[:, 0:1], ACT.Exp, scale=-2.0, name="splat_exp")
        k.act.act(amp, sc[:, 1:2], ACT.Exp, name="splat_exp")
        for a, b, o in ((ph, ph, pp), (dh, dh, dd), (ph, dh, pd)):
            v.tt(tmp[:], a[:], b[:], ALU.mult, name="v")
            v.wait("v")
            v.reduce(o, tmp[:], ALU.add, name="v")
            v.wait("v")
        k.act.wait("v")
        k.act.act(dd, dd, ACT.Sqrt, name="splat_norm")
        v.wait("splat_norm", "splat_exp")
        v.ts(dd, dd, 1e-8, ALU.add, name="v")
        v.wait("v")
        v.recip(inv_n, dd, name="v")
        v.stt(b_gauss, pp, -0.5, inv_s2, ALU.mult, ALU.mult, name="v")
        v.wait("v")
        v.stt(b_dir, pd, -1.0, inv_n, ALU.mult, ALU.mult, name="v")
        v.tt(amp, amp, sc[:, 3:4], ALU.mult, name="v")
        v.wait("v")
        strength = sc[:, 2:3]
        dims = [[k.ps("dims", [P, 512]) for _ in range(DC)] for _ in range(2)]
        gp, dp = [k.ps("gp", [P, 512]) for _ in range(2)], [k.ps("dp", [P, 512]) for _ in range(2)]
        raw, sq = ([[k.sb(n, [P, 512]) for _ in range(DC)] for _ in range(2)] for n in ("raw", "sq"))
        hi, lo = ([[k.sb(n, [P, 512], F32R) for _ in range(DC)] for _ in range(2)] for n in ("hi", "lo"))
        g, th, f1, f2 = ([k.sb(n, [P, 512]) for _ in range(2)] for n in ("g", "t", "f1", "f2"))
        fs = [[k.sb("fs", [P, 512], F32R) for _ in range(4)] for _ in range(2)]
        k.p.loop(NB)
        for s, scratch in ((0, k.rec_q), (1, k.rec_k)):
            tag, scale = "qk"[s], (HD ** -0.5, 1.0)[s]
            for c in range(DC):
                n = f"{tag}{c}"
                k.pe.wait(f"{n}_sq")
                k.pe.products(dims[s][c][:], three(
                    lambda a, s=s, c=c: wh[:, a, s * D + c * P:s * D + (c + 1) * P],
                    lambda a, s=s, c=c: wl[:, a, s * D + c * P:s * D + (c + 1) * P],
                    lambda a: lambda i, a=a: xh[:, a, ds(i * 512, 512)],
                    lambda a: lambda i, a=a: xl[:, a, ds(i * 512, 512)]), name=f"{n}_dims")
                k.act.wait(f"{n}_dims", f"{tag}_gauss_in", f"{tag}_dir_in", f"{n}_lo")
                k.act.act(raw[s][c][:], dims[s][c][:], name=f"{n}_raw")
                k.act.act(sq[s][c][:], dims[s][c][:], ACT.Square, name=f"{n}_sq")
                v.wait(f"{n}_raw", f"{n}_sent")
                v.ts(hi[s][c][:], raw[s][c][:], scale, ALU.mult, name=f"{n}_hi")
                v.wait(f"{n}_hi")
                v.stt(lo[s][c][:], raw[s][c][:], scale, f32(hi[s][c][:]), ALU.mult, ALU.subtract, name=f"{n}_lo")
                k.sp.wait(f"{n}_lo")
                for r, t in ((0, hi), (HD, lo)):
                    k.sp.dma(lambda i, c=c, r=r, scratch=scratch: scratch[
                        ds((i // 2) * H + c * 8, 8), r:r + HD, ds((i % 2) * 512, 512)], f32(t[s][c][:]),
                        k.dma_counter(f"{n}_sent"), f"{n}_sent")
            k.pe.wait(f"{tag}_g", f"{tag}0_sq", f"{tag}1_sq", f"{tag}0_raw", f"{tag}1_raw")
            k.pe.products(gp[s][:], [(half[:, c, :], sq[s][c][:]) for c in range(DC)]
                          + [(pos[:, c, :], raw[s][c][:]) for c in range(DC)], name=f"{tag}_gauss_in")
            k.pe.wait(f"{tag}_t")
            k.pe.products(dp[s][:], [(dirs[:, c, :], raw[s][c][:]) for c in range(DC)], name=f"{tag}_dir_in")
            k.act.wait(f"{tag}_gauss_in", f"{tag}_f1", f"{tag}_f2")
            k.act.act(g[s][:], gp[s][:], ACT.Exp, bias=b_gauss, scale=inv_s2, name=f"{tag}_g")
            k.act.wait(f"{tag}_dir_in")
            k.act.act(th[s][:], dp[s][:], ACT.Tanh, bias=b_dir, scale=inv_n, name=f"{tag}_t")
            v.wait(f"{tag}_g", f"{tag}_t", f"{tag}_sent", f"{tag}_split")
            if s == 0:
                v.ts(f1[s][:], g[s][:], amp, ALU.mult, name=f"{tag}_f1")
                v.wait(f"{tag}_f1")
                v.stt(f2[s][:], f1[s][:], strength, th[s][:], ALU.mult, ALU.mult, name=f"{tag}_f2")
            else:
                v.copy(f1[s][:], g[s][:], name=f"{tag}_f1")
                v.tt(f2[s][:], g[s][:], th[s][:], ALU.mult, name=f"{tag}_f2")
            v.wait(f"{tag}_f2")
            v.copy(fs[s][0][:], f1[s][:], name=f"{tag}_fh")
            v.copy(fs[s][1][:], f2[s][:], name=f"{tag}_fh")
            v.wait(f"{tag}_fh")
            v.tt(fs[s][2][:], f1[s][:], f32(fs[s][0][:]), ALU.subtract, name=f"{tag}_split")
            v.tt(fs[s][3][:], f2[s][:], f32(fs[s][1][:]), ALU.subtract, name=f"{tag}_split")
            k.sp.wait(f"{tag}_split")
            for r in range(4):
                k.sp.dma(lambda i, r=r, scratch=scratch: scratch[
                    ds((i // 2) * H, H), 2 * HD + r * NS:2 * HD + (r + 1) * NS, ds((i % 2) * 512, 512)],
                    f32(fs[s][r][:]), k.dma_counter(f"{tag}_sent"), f"{tag}_sent")
        k.p.end_loop()


def attention(k, kinds, blend):
    vals, heads = k.vals, k.heads
    nk = len(kinds)
    with scope(k):
        qs = [{kind: k.sb("q_" + kind, [P, S], F32R) for kind in kinds} for _ in range(2)]
        ks = [k.sb("keys", [P, S], F32R) for _ in range(2)]
        vb = [k.sb("values", [P, QT, 32]) for _ in range(2)]
        negmax = [{kind: k.sb("negmax", [P, QT]) for kind in kinds} for _ in range(2)]
        low = [k.sb("p_low", [P, 4, 512]) for _ in range(2)]
        high = [k.sb("p_high", [P, 2, 512]) for _ in range(2)]
        strip = [k.sb("strip", [P, 512]) for _ in range(2)]
        rows = k.sb("rows", [P, 512])
        rec, tmp = k.sb("rec", [P, 4, 2 * nk]), k.sb("tmp", [P, 4, 2 * nk, HD])
        wts = k.sb("wts", [P, 4, 2 * nk])
        px = k.ps("px", [P, 2, 512])
        pss = k.ps("pss", [P, 4, 512])
        po, pr = k.ps("po", [P, 512]), k.ps("pr", [P, 512])
        pool, pe, act, v, sp = k.pool, k.pe, k.act, k.dve, k.sp
        for p in range(2):
            pool.memset(f32(ks[p][:]), 0.0, name="clear")
            for kind in kinds:
                pool.memset(f32(qs[p][kind][:]), 0.0, name="clear")
            pool.memset(low[p][:], 0.0, name="clear")
        pool.memset(rows[:], 0.0, name="clear")
        pool.wait("clear")
        for p in range(2):
            pool.memset(f32(ks[p][KROW:KROW + 1, :]), 1.0, name="clear")
        pool.wait("clear")
        for n in range(nk):
            pool.copy(wts[:, :, 2 * n:2 * n + 2], blend[n], name="clear")
        k.p.barrier()

        def load(u, p):
            def rec(t, a, b):
                return lambda i: t[ds(u(i), 1), a:b, :]
            sp.wait(f"used{p}")
            parts = []
            for kind in kinds:
                parts += [(qs[p][kind], 0, k.rec_q, 0, 32), (qs[p][kind], 32, k.rec_q, 0, 16)]
            parts += [(ks[p], 0, k.rec_k, 0, 16), (ks[p], 16, k.rec_k, 0, 32)]
            if "gsa" in kinds:
                parts += [(qs[p]["gsa"], 48, k.rec_q, 32, 64), (qs[p]["gsa"], 80, k.rec_q, 32, 48),
                          (ks[p], 48, k.rec_k, 32, 48), (ks[p], 64, k.rec_k, 32, 64)]
            for t, r, src, a, b in parts:
                sp.dma(f32(t[r:r + b - a, :]), rec(src, a, b), k.dma_counter(f"head{p}"), f"head{p}")
            pool.wait(f"used{p}")
            pool.copy(vb[p][:], lambda i: vals[:, ds((u(i) // H) * QT, QT), ds(u(i) % H, 1), :],
                      name=f"values{p}")

        def maxima(p):
            for kind in kinds:
                for t in range(QT):
                    banks = (t % 2,) if t < 4 else (0, 1)
                    pe.wait(f"head{p}", *(f"x_read{b}" for b in banks))
                    q = qs[p][kind][0:KROW, t * P:(t + 1) * P]
                    width = (t + 1) * P
                    for n, c in enumerate(range(0, width, 512)):
                        w = min(512, width - c)
                        bank = px[:, banks[n], :]
                        diag = c + w == width
                        pe.mm(bank[:, 0:w], q, ks[p][0:KROW, c:c + w], True, not diag)
                        if diag:
                            pe.mm(bank[:, w - P:w], k.identb[:], k.mask_q[:], False, True, name=f"x{p}")
                    v.wait(f"x{p}", f"max_turned{p}")
                    src = px[:, banks[0], 0:width] if t < 4 else \
                        px[:].rearrange("p b w -> p (b w)")[:, 0:width]
                    v.reduce(negmax[p][kind][:, t:t + 1], src, ALU.max, negate=True, name=f"x_read{banks[0]}")
                    if t >= 4:
                        k.p.alias("x_read1", "x_read0")
                    k.p.alias(f"negmax{p}", f"x_read{banks[0]}")
                    yield

        def head(u, p, other=None, start=0, rate=2):
            pe.wait(f"negmax{p}", "exp0", "exp1")
            for n, kind in enumerate(kinds):
                for t in range(QT):
                    pe.mm(pss[KROW:KROW + 1, 2 * n + t // 4, (t % 4) * P:(t % 4 + 1) * P],
                          negmax[p][kind][:, t:t + 1], k.ident[:], name=f"max_turned{p}")
            for n, kind in enumerate(kinds):
                act.wait(f"max_turned{p}")
                act.act(qs[p][kind][KROW:KROW + 1, :].rearrange("r (b w) -> r b w", b=2),
                        pss[KROW:KROW + 1, 2 * n:2 * n + 2, :], name=f"max_row{n}")
            steps = [(n, half, j) for n in range(nk) for half in range(2) for j in range(0, 4 * (half + 1), 2)]
            todo = []

            def weights(n, half, j, s):
                kind = kinds[n]
                pe.wait(f"exp{s % 2}", *(f"max_row{m}" for m in range(nk)))
                spans = []
                for m in range(2):
                    q0 = max(half * 512, (j + m) * P)
                    w = (half + 1) * 512 - q0
                    diag = (j + m) * P >= half * 512
                    out = pss[:, 2 * (s % 2) + m, 512 - w:512]
                    pe.mm(out, ks[p][0:STACK, (j + m) * P:(j + m + 1) * P], qs[p][kind][0:STACK, q0:q0 + w],
                          True, not diag, name=None if diag else f"scores{s % 2}")
                    if diag:
                        pe.mm(pss[:, 2 * (s % 2) + m, 512 - w:512 - w + P], k.identb[:], k.mask_k[:],
                              False, True, name=f"scores{s % 2}")
                    spans.append(w)
                turn = (p * nk + n) % 2
                buf = low[turn][:, j:j + 2, :] if half == 0 else high[s % 2][:]
                act.wait(f"scores{s % 2}", f"low_read{turn}" if half == 0 else f"high_read{s % 2}")
                if spans[0] == spans[1]:
                    act.act(buf, pss[:, 2 * (s % 2):2 * (s % 2) + 2, :], ACT.Exp, name=f"exp{s % 2}")
                else:
                    for m in range(2):
                        w = spans[m]
                        act.act(buf[:, m, 512 - w:512], pss[:, 2 * (s % 2) + m, 512 - w:512], ACT.Exp,
                                name=f"exp{s % 2}")
                return buf, spans, turn

            def values(n, half, j, s, buf, spans, turn):
                pe.wait(f"exp{s % 2}", f"values{p}")
                if j == 0:
                    pe.wait("po_read")
                for m in range(2):
                    jj = j + m
                    c = 32 * (jj % 4)
                    w = 512 if half == 0 else spans[m]
                    mark = f"low_read{turn}" if half == 0 else f"high_read{s % 2}"
                    pe.mm(po[c:c + 32, 512 - w:512], vb[p][:, jj, :], buf[:, m, 512 - w:512],
                          jj < 4, half == 0 or jj >= 4, name=mark if m == 1 else None)
                if j == 4 * (half + 1) - 2:
                    k.p.alias("po", mark)
                    v.wait("po", f"strip_read{half}")
                    v.copy(strip[half][:], po[:], name="po_read")
                    todo.append((n, half))

            def fold(n, half):
                pe.wait("po_read")
                if n == 0 and half == 0:
                    pe.wait("out_read")
                r = 32 * (2 * n + half)
                pe.mm(pr[r:r + 32, :], k.strips[:], strip[half][:], name=f"strip_read{half}")

            behind = None
            for s, step in enumerate(steps):
                now = (*step, s, *weights(*step, s))
                if other is not None and s >= start:
                    for _ in range(rate):
                        next(other, None)
                if behind:
                    while todo:
                        fold(*todo.pop(0))
                    values(*behind)
                behind = now
            while todo:
                fold(*todo.pop(0))
            values(*behind)
            k.p.alias(f"used{p}", "high_read1")
            if other is not None:
                for _ in other:
                    pass
            while todo:
                fold(*todo.pop(0))
            rw = 64 * nk
            act.wait(f"strip_read1", "rows_read")
            act.act(rows[0:rw, :], pr[0:rw, :], name="rows")
            pe.wait("rows")
            outv = pr[:].rearrange("p (t r) -> p t r", t=4)
            for t in range(4):
                pe.transpose(outv[:, t, :], rows[:, t * P:(t + 1) * P], k.ident[:], name="rows_read")
            v.wait("rows_read", "tmp_read")
            ov = pr[:].rearrange("p (t m r) -> p t m r", t=4, m=4)[:, :, 0:2 * nk, :]
            v.recip(rec[:], ov[:, :, :, HD], name="rec")
            v.wait("rec")
            v.tt(rec[:], rec[:], wts[:], ALU.mult, name="rec")
            v.wait("rec")
            for t in range(4):
                v.tt(tmp[:, t], ov[:, t, :, 0:HD], rec[:, t].unsqueeze(2).to_broadcast([P, 2 * nk, HD]),
                     ALU.mult, name="out_read")
            pool.wait("out_read")
            for half in range(2):
                dst = lambda i, half=half: heads[:, ds(u(i), 1), half * 4:half * 4 + 4, :]
                if nk == 2:
                    pool.tt(dst, tmp[:, :, half, :], tmp[:, :, 2 + half, :], ALU.add, name="tmp_read")
                else:
                    pool.copy(dst, tmp[:, :, half, :], name="tmp_read")

        def run(gen):
            for _ in gen:
                pass

        first = 4 if nk == 2 else 2
        load(lambda i: 0, 0)
        load(lambda i: 1, 1)
        run(maxima(0))
        k.p.loop(B * H // 2 - 1)
        head(lambda i: 2 * i, 0, maxima(1))
        load(lambda i: 2 * i + 2, 0)
        head(lambda i: 2 * i + 1, 1, maxima(0), first, 2)
        load(lambda i: 2 * i + 3, 1)
        k.p.end_loop()
        last = B * H - 2
        head(lambda i: last, 0, maxima(1))
        head(lambda i: last + 1, 1)


def swiglu(k):
    xh, xl = k.xh, k.xl
    with scope(k):
        gw, uw = (k.sb(n, [P, DC, F0], F32R) for n in ("gw", "uw"))
        dw = k.sb("dw", [P, FC, D])
        gs, us, dsc = k.sb("gs", [P, FC]), k.sb("us", [P, FC]), k.sb("dsc", [P, D])
        with scope(k):
            raw = [k.sb("raw", [P, DC * F0]) for _ in range(3)]
            unit = k.sb("unit", [P, DC * F0])
            k.load((raw[0][:], "gate_w"), (raw[1][:], "up_w"), (raw[2][:], "down_w"), (gs[:], "gate_s"),
                   (us[:], "up_s"), (dsc[:], "down_s"))
            k.p.barrier()
            v = k.dve
            for w, out in zip(raw, (gw[:].rearrange("p c f -> p (c f)"), uw[:].rearrange("p c f -> p (c f)"),
                                    dw[:].rearrange("p c f -> p (c f)"))):
                v.wait("v")
                v.ts(unit[:].bitcast(U32), w[:].bitcast(U32), 0x7F800000, ALU.bitwise_and, name="v")
                v.wait("v")
                v.ts(unit[:], unit[:], 2.0 ** -6, ALU.max, 1.5 * 2.0 ** 20, ALU.mult, name="v")
                v.wait("v")
                v.tt(w[:], w[:], unit[:], ALU.add, name="v")
                v.wait("v")
                v.tt(w[:], w[:], unit[:], ALU.subtract, name="v")
                v.wait("v")
                v.stt(unit[:], w[:], -1.0, w[:], ALU.mult, ALU.max, name="v")
                v.wait("v")
                v.ts(unit[:], unit[:], 448.0, ALU.is_gt, 3.0e38, ALU.mult, name="v")
                v.wait("v")
                v.ts(unit[:], unit[:], 3.0e38, ALU.mult, name="v")
                v.wait("v")
                v.tt(out, w[:], unit[:], ALU.add, name="v")
        pg, pu = [k.ps("pg", [P, 512]) for _ in range(2)], [k.ps("pu", [P, 512]) for _ in range(2)]
        py = [k.ps("py", [P, D]) for _ in range(2)]
        sg = [k.sb("sg", [P, 512]) for _ in range(2)]
        fz = k.sb("fz", [P, FC, 512])
        y = [k.sb("y", [P, D]) for _ in range(2)]
        k.p.loop(NB)
        for f in range(FC):
            b = f % 2
            for w, out, n in ((gw, pg[b], "g"), (uw, pu[b], "u")):
                k.pe.wait(f"silu{b}" if n == "g" else f"fused{b}")
                k.pe.products(out[:], [(w[:, c, f * P:(f + 1) * P],
                                        lambda i, c=c, x=x: x[:, c, ds(i * 512, 512)])
                                       for c in range(DC) for x in (xh, xl)], name=f"{n}{b}")
            k.act.wait(f"g{b}", f"fused{b}")
            k.act.act(sg[b][:], pg[b][:], ACT.Silu, scale=gs[:, f:f + 1], name=f"silu{b}")
            k.dve.wait(f"silu{b}", f"u{b}", "down1", "down0")
            k.dve.stt(fz[:, f, :], pu[b][:], us[:, f:f + 1], sg[b][:], ALU.mult, ALU.mult, name=f"fused{b}")
        for t in range(4):
            b = t % 2
            k.pe.wait("fused0", "fused1", f"scaled{b}")
            k.pe.products(py[b][:], [(fz[:, f, t * P:(t + 1) * P], dw[:, f, :]) for f in range(FC)], name=f"down{b}")
            k.dve.wait(f"down{b}", f"added{b}")
            k.dve.tt(y[b][:], py[b][:], dsc[:], ALU.mult, name=f"scaled{b}")
            k.dve.wait(f"scaled{b}")
            k.dve.tt(lambda i, t=t: k.x[:, ds(4 * i + t, 1), :], lambda i, t=t: k.x[:, ds(4 * i + t, 1), :],
                     y[b][:], ALU.add, name=f"added{b}")
        k.p.end_loop()


def output_projection(k, weight, into):
    heads = k.heads
    with scope(k):
        w = k.sb("wo", [P, DC, D])
        k.load((w[:], weight))
        k.p.barrier()
        o = [k.sb("o", [P, D]) for _ in range(2)]
        ot = [k.sb("ot", [P, DC, P]) for _ in range(2)]
        pt, py = [k.ps("pt", [P, DC, P]) for _ in range(2)], [k.ps("py", [P, D]) for _ in range(2)]
        k.p.loop(NT // 2)
        for p in range(2):
            k.pool.wait(f"turned{p}")
            k.pool.copy(o[p][:].rearrange("p (h d) -> p h d", h=H),
                        lambda i, p=p: heads[:, ds(((2 * i + p) // QT) * H, H), ds((2 * i + p) % QT, 1), :],
                        name=f"o{p}")
            k.pe.wait(f"o{p}", f"ot{p}")
            for c in range(DC):
                k.pe.transpose(pt[p][:, c, :], o[p][:, c * P:(c + 1) * P], k.ident[:], name=f"turned{p}")
            k.act.wait(f"turned{p}", f"y{p}")
            k.act.act(ot[p][:], pt[p][:], name=f"ot{p}")
            k.pe.wait(f"ot{p}", f"added{p}")
            k.pe.products(py[p][:], [(ot[p][:, c, :], w[:, c, :]) for c in range(DC)], name=f"y{p}")
            k.dve.wait(f"y{p}")
            k.dve.tt(lambda i, p=p: into[:, ds(2 * i + p, 1), :], lambda i, p=p: into[:, ds(2 * i + p, 1), :],
                     py[p][:], ALU.add, name=f"added{p}")
        k.p.end_loop()


def normalised_transpose(k, src, scale_col, dst, shift=None, features=None):
    xn = [k.sb("xn", [P, D]) for _ in range(2)]
    th = [k.sb("th", [P, DC, P], F32R) for _ in range(2)]
    tl = [k.sb("tl", [P, DC, P], F32R) for _ in range(2)]
    pt = [k.ps("pt", [P, DC, P]) for _ in range(2)]
    k.p.loop(NT // 2)
    for p in range(2):
        k.dve.wait(f"turned{p}")
        k.dve.ts(xn[p][:], lambda i, p=p: src[:, ds(2 * i + p, 1), :],
                 lambda i, p=p: scale_col[:, ds(2 * i + p, 1)], ALU.mult, name=f"xn{p}")
        transposed_tile(k, p, xn, pt, th, tl, scale=features)
    k.p.end_loop()


def second_norm(k):
    with scope(k):
        mean, var = moments(k, k.x, "ln1")
        inverse_root(k, var, "ln1")
        for t in range(NT):
            k.dve.ts(k.h[:, t, :], k.x[:, t, :], mean[:, t:t + 1], ALU.subtract, var[:, t:t + 1], ALU.mult, name="v")
        k.dve.wait("v")
        mean2, var2 = moments(k, k.h, "ln1b")
        k.dve.copy(k.hop_mean[:], mean2[:], name="v")
        k.dve.copy(k.hop_scale[:], var2[:], name="v")
        k.dve.tt(mean2[:], mean2[:], mean2[:], ALU.mult, name="v")
        k.dve.wait("v")
        k.dve.tt(k.rms[:], mean2[:], var2[:], ALU.add, name="v")
        k.dve.wait("v")
        inverse_root(k, k.hop_scale, "hop")
        inverse_root(k, k.rms, "rms")


def latent_projections(k):
    xh, xl, vals = k.xh, k.xl, k.vals
    with scope(k):
        names = (("wd", "lat_down", [P, DC, P]), ("qa", "lat_qa", [P, D]), ("qb", "lat_qb", [P, D]),
                 ("kd", "lat_kd", [P, D]), ("ka", "lat_ka", [P, DC, D]), ("kb", "lat_kb", [P, DC, D]),
                 ("vu", "lat_v", [P, D]))
        hi, lo = {}, {}
        raws = []
        for n, src, shape in names:
            hi[n], lo[n] = k.sb(n + "h", shape, F32R), k.sb(n + "l", shape, F32R)
        cos, sin, ln1 = k.sb("cos", [P, T]), k.sb("sin", [P, T]), k.sb("ln1", [P, DC])
        with scope(k):
            for n, src, shape in names:
                raws.append((n, k.sb(n, shape), src))
            k.load(*((r[:], src) for _, r, src in raws), (cos[:], "rope_cos"), (sin[:], "rope_sin"), (ln1[:], "ln1_w"))
            k.p.barrier()
            for n, r, _ in raws:
                k.split(hi[n][:], lo[n][:], r[:], n)
        with scope(k):
            normalised_transpose(k, k.h, k.rms, None, features=ln1)
        k.pool.memset(vals[:], 0.0, name="vals0")
        k.pool.wait("vals0")
        k.pool.memset(vals[:, :, :, HD:HD + 1], 1.0, name="vals1")
        v = k.dve
        dh, dl = k.sb("dh", [P, 512], F32R), k.sb("dl", [P, 512], F32R)
        pd = k.ps("pd", [P, 512])
        pa, pb = [k.ps("pa", [P, 512]) for _ in range(2)], [k.ps("pb", [P, 512]) for _ in range(2)]
        pv = [k.ps("pv", [P, D]) for _ in range(2)]
        ta, tb = [k.sb("ta", [P, 512]) for _ in range(2)], [k.sb("tb", [P, 512]) for _ in range(2)]
        th, tl = [k.sb("oh", [P, 512], F32R) for _ in range(2)], [k.sb("ol", [P, 512], F32R) for _ in range(2)]

        def xs(w, c0):
            return three(lambda a: hi[w][:, a, c0:c0 + P], lambda a: lo[w][:, a, c0:c0 + P],
                         lambda a: lambda i, a=a: xh[:, a, ds(i * 512, 512)],
                         lambda a: lambda i, a=a: xl[:, a, ds(i * 512, 512)])

        def lat(w, c0, n=P, t=None):
            a, b = hi[w][:, c0:c0 + n], lo[w][:, c0:c0 + n]
            if t is None:
                return [(a, dh[:]), (b, dh[:]), (a, dl[:])]
            c, d = dh[:, t * P:(t + 1) * P], dl[:, t * P:(t + 1) * P]
            return [(c, a), (c, b), (d, a)]

        k.p.loop(NB)
        k.pe.wait("dh", "dl")
        k.pe.products(pd[:], xs("wd", 0), name="down")
        k.act.wait("down", "b1", "v1")
        k.act.act(dh[:], pd[:], name="dh")
        v.wait("dh", "b1", "v1")
        v.tt(dl[:], pd[:], f32(dh[:]), ALU.subtract, name="dl")
        for n, (s, c) in enumerate(((0, 0), (0, 1), (1, 0), (1, 1))):
            b = n % 2
            scratch, scale = ((k.rec_q, HD ** -0.5), (k.rec_k, 1.0))[s]
            c0 = c * P
            k.pe.wait("dl", "dh", f"ta{b}")
            k.pe.products(pa[b][:], lat("qa", c0) if s == 0 else lat("kd", c0) + xs("ka", c0), name=f"a{b}")
            k.pe.wait(f"tb{b}")
            k.pe.products(pb[b][:], lat("qb", c0) if s == 0 else xs("kb", c0), name=f"b{b}")
            v.wait(f"a{b}", f"b{b}", f"sent{b}", f"tl{b}")
            v.tt(ta[b][:], pa[b][:], lambda i: cos[:, ds(i * 512, 512)], ALU.mult, name=f"ta{b}")
            v.tt(tb[b][:], pb[b][:], lambda i: sin[:, ds(i * 512, 512)], ALU.mult, name=f"tb{b}")
            v.wait(f"ta{b}", f"tb{b}")
            v.tt(ta[b][:], ta[b][:], tb[b][:], ALU.add, name=f"sum{b}")
            v.wait(f"sum{b}")
            v.ts(th[b][:], ta[b][:], scale, ALU.mult, name=f"th{b}")
            v.wait(f"th{b}")
            v.stt(tl[b][:], ta[b][:], scale, f32(th[b][:]), ALU.mult, ALU.subtract, name=f"tl{b}")
            k.sp.wait(f"tl{b}")
            for r, t in ((0, th), (HD, tl)):
                k.sp.dma(lambda i, c=c, r=r, scratch=scratch: scratch[
                    ds((i // 2) * H + c * 8, 8), r:r + HD, ds((i % 2) * 512, 512)], f32(t[b][:]),
                    k.dma_counter(f"lat{b}"), f"sent{b}")
        for t in range(4):
            b = t % 2
            k.pe.wait(f"v_out{b}")
            k.pe.products(pv[b][:], lat("vu", 0, D, t), name=f"v{b}")
            k.act.wait(f"v{b}")
            k.act.act(lambda i, t=t: vals[:, ds(4 * i + t, 1), :, 0:HD],
                      pv[b][:].rearrange("p (o h d) -> p o h d", o=1, h=H), name=f"v_out{b}")
        k.p.end_loop()


def experts(k):
    xh, xl = k.xh, k.xl
    with scope(k):
        gh, gl, uh, ul = (k.sb(n, [P, DC, NE * P], F32R) for n in ("gh", "gl", "uh", "ul"))
        dw = k.sb("dw", [P, NE, D])
        rw, rb, ln2 = k.sb("rw", [P, DC, 64]), k.sb("rb", [P, NR]), k.sb("ln2", [P, DC])
        with scope(k):
            g, u = k.sb("g", [P, DC, NE * P]), k.sb("u", [P, DC, NE * P])
            k.load((g[:], "moe_gate"), (u[:], "moe_up"), (dw[:], "moe_down"), (rw[:], "router_w"),
                   (rb[:], "router_b"), (ln2[:], "ln2_w"))
            k.p.barrier()
            k.split(gh[:], gl[:], g[:], "g")
            k.split(uh[:], ul[:], u[:], "u")
        with scope(k):
            mean, var = moments(k, k.h, "rms2")
            k.dve.tt(mean[:], mean[:], mean[:], ALU.mult, name="v")
            k.dve.wait("v")
            k.dve.tt(k.rms[:], mean[:], var[:], ALU.add, name="v")
            k.dve.wait("v")
            inverse_root(k, k.rms, "rms2")
            normalised_transpose(k, k.h, k.rms, None, features=ln2)
        probs, top = k.sb("probs", [P, NT, 8]), k.sb("top", [P, NT, 8])
        wts, picked = k.sb("wts", [P, NT, 8]), k.sb("picked", [P, NT, 8])
        idx, idxf = k.sb("idx", [P, NT, 8], U32), k.sb("idxf", [P, NT, 8])
        number = k.sb("number", [P, NT, 8])
        total = k.sb("total", [P, NT])
        v = k.dve
        with scope(k):
            pl = [k.ps("pl", [P, 64]) for _ in range(2)]
            xs = [k.sb("xs", [P, DC, P]) for _ in range(2)]
            v.memset(probs[:], -1.0, name="v")
            v.memset(number[:], 0.0, name="v")
            for e in range(1, NE):
                v.wait("v")
                v.memset(number[:, :, e], float(e), name="v")
            k.p.loop(NT // 2)
            for p in range(2):
                v.wait(f"l{p}")
                v.tt(xs[p][:], lambda i, p=p: f32(xh[:, :, ds((2 * i + p) * P, P)]),
                     lambda i, p=p: f32(xl[:, :, ds((2 * i + p) * P, P)]), ALU.add, name=f"xs{p}")
                k.pe.wait(f"xs{p}", f"lr{p}")
                k.pe.products(pl[p][:], [(xs[p][:, c, :], rw[:, c, :]) for c in range(DC)], name=f"l{p}")
                v.wait(f"l{p}")
                v.tt(lambda i, p=p: probs[:, ds(2 * i + p, 1), 0:NR], pl[p][:, 0:NR], rb[:], ALU.add, name=f"lr{p}")
            k.p.end_loop()
            lg = probs[:, :, 0:NR]
            k.act.act(lg, lg, ACT.Exp, scale=-1.0, name="sig")
            v.wait("sig")
            v.ts(lg, lg, 1.0, ALU.add, name="v")
            v.wait("v")
            v.recip(lg, lg, name="v")
            v.wait("v")
            for t in range(NT):
                v.op(lambda e, i, t=t: e.max(top[:, t, :], probs[:, t, :]), "v")
            v.wait("v")
            for t in range(NT):
                v.op(lambda e, i, t=t: e.max_index(idx[:, t, :], top[:, t, :], probs[:, t, :]), "v")
            v.wait("v")
            v.copy(idxf[:], idx[:], name="v")
            v.tt(total[:], top[:, :, 0], top[:, :, 1], ALU.add, name="v")
            v.wait("v")
            v.recip(total[:], total[:], name="v")
            v.wait("v")
            for s in range(2):
                v.tt(top[:, :, s], top[:, :, s], total[:], ALU.mult, name="v")
                v.tt(picked[:], number[:], idxf[:, :, s:s + 1].to_broadcast([P, NT, 8]), ALU.is_equal, name="v")
                v.wait("v")
                out = wts if s == 0 else picked
                v.tt(out[:], picked[:], top[:, :, s:s + 1].to_broadcast([P, NT, 8]), ALU.mult, name="v")
                v.wait("v")
            v.tt(wts[:], wts[:], picked[:], ALU.add, name="v")
            v.wait("v")
            v.ts(wts[:], wts[:], 0.125, ALU.mult, name="v")
            v.memset(total[:], 0.125, name="v")
        pg, pu = [k.ps("pg", [P, 512]) for _ in range(2)], [k.ps("pu", [P, 512]) for _ in range(2)]
        py = [k.ps("py", [P, D]) for _ in range(4)]
        sg = [k.sb("sg", [P, 512]) for _ in range(2)]
        hz = [k.sb("hz", [P, 512]) for _ in range(2)]
        k.p.loop(NB)
        for t in range(4):
            v.tt(lambda i, t=t: k.x[:, ds(4 * i + t, 1), :], lambda i, t=t: k.x[:, ds(4 * i + t, 1), :],
                 lambda i, t=t: k.h[:, ds(4 * i + t, 1), :], ALU.add, name=f"y_added{t}")
        behind = None

        def down(e, b):
            for t in range(4):
                k.pe.wait(f"fused{b}", f"y_read{t}")
                k.pe.mm(py[t][:], hz[b][:, t * P:(t + 1) * P], dw[:, e, :], name=f"y{t}")
                k.p.alias(f"down{b}", f"y{t}")
                v.wait(f"y{t}", f"y_added{t}")
                col = (lambda i, t=t: total[:, ds(4 * i + t, 1)]) if e == 0 else \
                    (lambda i, t=t, e=e: wts[:, ds(4 * i + t, 1), e - 1])
                v.stt(lambda i, t=t: k.x[:, ds(4 * i + t, 1), :], py[t][:], col,
                      lambda i, t=t: k.x[:, ds(4 * i + t, 1), :], ALU.mult, ALU.add, name=f"y_read{t}")
                k.p.alias(f"y_added{t}", f"y_read{t}")

        for e in range(NE):
            b = e % 2
            for wh, wl, out, n in ((gh, gl, pg[b], "g"), (uh, ul, pu[b], "u")):
                k.pe.wait(f"silu{b}" if n == "g" else f"fused{b}")
                k.pe.products(out[:], three(
                    lambda c: wh[:, c, e * P:(e + 1) * P], lambda c: wl[:, c, e * P:(e + 1) * P],
                    lambda c: lambda i, c=c: xh[:, c, ds(i * 512, 512)],
                    lambda c: lambda i, c=c: xl[:, c, ds(i * 512, 512)]), name=f"{n}{b}")
            k.act.wait(f"g{b}", f"fused{b}")
            k.act.act(sg[b][:], pg[b][:], ACT.Silu, name=f"silu{b}")
            v.wait(f"silu{b}", f"u{b}", f"down{b}")
            v.tt(hz[b][:], pu[b][:], sg[b][:], ALU.mult, name=f"fused{b}")
            if behind:
                down(*behind)
            behind = (e, b)
        down(*behind)
        k.p.end_loop()


def hopfield_weights(k):
    with scope(k):
        mem = k.sb("mem", [P, MC, P])
        wq, wk, wv, wo = k.sb("wq", [P, HH, D]), k.sb("wk", [P, HH, P]), k.sb("wv", [P, HH, P]), k.sb("wo", [P, HH, D])
        gm, bm, beta = k.sb("gm", [P, 1]), k.sb("bm", [P, 1]), k.sb("beta", [P, HH])
        k.load((mem[:], "memory"), (wq[:], "hop_q"), (wk[:], "hop_k"), (wv[:], "hop_v"), (wo[:], "hop_o"),
               (gm[:], "g_mem"), (bm[:], "b_mem"), (beta[:], "log_beta"))
        k.p.barrier()
        k.act.act(beta[:], beta[:], ACT.Exp, name="beta")
        v, pe = k.dve, k.pe
        v.wait("beta")
        v.ts(beta[:], beta[:], 0.5, ALU.mult, name="v")
        mean, var = moments(k, mem, "mem", MC, P)
        inverse_root(k, var, "mem")
        mn, mt = k.sb("mn", [P, MC, P]), k.sb("mt", [P, NM])
        pt = k.ps("pt", [P, NM])
        for m in range(MC):
            v.ts(mn[:, m, :], mem[:, m, :], mean[:, m:m + 1], ALU.subtract, var[:, m:m + 1], ALU.mult, name="v")
        pe.wait("v")
        for m in range(MC):
            pe.transpose(pt[:, m * P:(m + 1) * P], mn[:, m, :], k.ident[:], name="mem_turned")
        v.wait("mem_turned")
        v.ts(mt[:], pt[:], gm[:], ALU.mult, bm[:], ALU.add, name="mt")
        kt, vt = [k.sb("kt", [P, NM]) for _ in range(2)], [k.sb("vt", [P, NM]) for _ in range(2)]
        pk, pv = k.ps("pk", [P, NM]), k.ps("pv", [P, NM])
        pa = [k.ps("pa", [P, 2, D]) for _ in range(3)]
        pe.wait("mt")
        for h in range(HH):
            b = h % 2
            pe.wait("kt0", "kt1", "vt0", "vt1")
            pe.mm(pk[:], wk[:, h, :], mt[:], name="k_in")
            pe.mm(pv[:], wv[:, h, :], mt[:], name="v_in")
            k.act.wait("k_in", f"c_in{b}")
            k.act.act(kt[b][:], pk[:], scale=beta[:, h:h + 1], name=f"kt{b}")
            v.wait("v_in", f"c_in{b}")
            v.copy(vt[b][:], pv[:], name=f"vt{b}")
            pe.wait(f"kt{b}", f"vt{b}", "a_out", "c_out")
            for n, (lhsT, rhs) in enumerate(((wq[:, h], kt[b]), (vt[b], kt[b]), (vt[b], wo[:, h]))):
                for m in range(2):
                    pe.mm(pa[n][:, m, :], lhsT[:, m * P:(m + 1) * P], rhs[:, :] if n < 2 else rhs,
                          name="c_in" + str(b) if n == 2 and m == 1 else None)
            k.act.wait(f"c_in{b}")
            v.wait(f"c_in{b}")
            k.act.act(k.to_scores[:, h], pa[0][:], name="a_out")
            k.act.act(k.again[:, h], pa[1][:], name="a_out")
            v.copy(k.to_out[:, h], pa[2][:], name="c_out")


def hopfield(k):
    with scope(k):
        gs, bs = k.sb("gs", [P, DC]), k.sb("bs", [P, DC])
        k.load((gs[:], "g_state"), (bs[:], "b_state"))
        k.p.barrier()
        pe, act, v, pool = k.pe, k.act, k.dve, k.pool
        xn = [k.sb("xn", [P, D]) for _ in range(2)]
        xt = [k.sb("xt", [P, DC, P]) for _ in range(2)]
        s = [k.sb("s", [P, HH, NM]) for _ in range(2)]
        r = [k.sb("r", [P, HH, NM]) for _ in range(2)]
        wt = [k.sb("wt", [P, MC, HH, P]) for _ in range(2)]
        cols = [k.sb("cols", [P, 8, HH]) for _ in range(2)]
        pss = [k.ps("pss", [P, 2, 2, NM]) for _ in range(2)]
        pt = [k.ps("pt", [P, 4, P]) for _ in range(2)]
        py = k.ps("py", [P, 512])
        pxt = k.ps("pxt", [P, DC, P])

        def state(p):
            v.wait(f"state{p}_in")
            v.ts(xn[p][:], lambda i: k.h[:, ds(2 * i + p, 1), :], lambda i: k.hop_mean[:, ds(2 * i + p, 1)],
                 ALU.subtract, lambda i: k.hop_scale[:, ds(2 * i + p, 1)], ALU.mult, name=f"state{p}")
            pe.wait(f"state{p}", "state_out")
            for c in range(DC):
                pe.transpose(pxt[:, c, :], xn[p][:, c * P:(c + 1) * P], k.ident[:], name=f"state{p}_in")
            v.wait(f"state{p}_in", f"scores_a{p}")
            for c in range(DC):
                v.ts(xt[p][:, c, :], pxt[:, c, :], gs[:, c:c + 1], ALU.mult, bs[:, c:c + 1], ALU.add, name="state_out")

        def scores(p, step):
            lhs, rhs = (xt[p][:, 0:DC].unsqueeze(2).to_broadcast([P, DC, 1, P]), k.to_scores) if step == 0 \
                else (wt[p], k.again)
            for q in range(4):
                half = q // 2
                pe.wait("state_out", f"weights{p}", f"s_out{half}")
                for h in range(2 * q, 2 * q + 2):
                    for c in range(2):
                        lhsT = xt[p][:, c, :] if step == 0 else wt[p][:, c, h, :]
                        pe.mm(pss[half][:, q % 2, h % 2, :], lhsT, rhs[:, h, c, :], c == 0, c == 1,
                              name=f"scores{half}")
                k.p.alias(f"scores_a{p}", f"scores{half}")
                if q % 2:
                    act.wait(f"scores{half}", f"s_read{p}")
                    act.act(s[p][:, 4 * half:4 * half + 4, :],
                            pss[half][:].rearrange("p a b n -> p (a b) n"), name=f"s_out{half}")
                    k.p.alias(f"s{p}", f"s_out{half}")

        def threshold(p):
            tau, neg, sq, root, total, slope = (cols[p][:, n, :] for n in range(6))
            v.wait(f"s{p}", f"tau_read{p}")
            v.reduce(tau, s[p][:], ALU.max, name=f"t{p}")
            v.wait(f"t{p}")
            v.ts(tau, tau, -1.0, ALU.add, name=f"t{p}")
            for n in range(NEWTON):
                v.wait(f"t{p}")
                v.ts(neg, tau, -1.0, ALU.mult, name=f"neg{p}")
                for h in range(HH):
                    v.wait(f"sq{p}_{h}", f"r_turned{p}")
                    v.ts(r[p][:, h, :], s[p][:, h, :], tau[:, h:h + 1], ALU.max, 0.0, ALU.add,
                         accum=total[:, h:h + 1], name=f"r{p}_{h}")
                    act.wait(f"r{p}_{h}", f"neg{p}", f"newton{p}")
                    act.act(r[p][:, h, :], r[p][:, h, :], ACT.Square, bias=neg[:, h:h + 1],
                            accum=sq[:, h:h + 1], name=f"sq{p}_{h}")
                act.wait(f"sq{p}_{HH - 1}")
                act.act(root, sq, ACT.Sqrt, name=f"root{p}")
                v.wait(f"r{p}_{HH - 1}")
                v.stt(slope, tau, -float(NM), total, ALU.mult, ALU.add, name=f"t{p}")
                v.wait(f"t{p}")
                v.recip(slope, slope, name=f"t{p}")
                v.wait(f"root{p}")
                v.tt(root, sq, root, ALU.subtract, name=f"newton{p}")
                v.wait(f"newton{p}", f"t{p}")
                v.tt(root, root, slope, ALU.mult, name=f"newton{p}")
                v.wait(f"newton{p}")
                v.tt(tau, tau, root, ALU.add, name=f"t{p}")
                yield
            v.wait(f"t{p}")
            for h in range(HH):
                v.wait(f"sq{p}_{h}", f"r_turned{p}")
                v.ts(r[p][:, h, :], s[p][:, h, :], tau[:, h:h + 1], ALU.subtract, 0.0, ALU.max, name=f"r{p}_{h}")
            k.p.alias(f"s_read{p}", f"r{p}_{HH - 1}")
            k.p.alias(f"tau_read{p}", f"r{p}_{HH - 1}")
            yield

        def weights(p):
            for g in range(4):
                b = g % 2
                pe.wait(f"r{p}_{2 * g + 1}", f"w_out{b}")
                for c in range(2):
                    for h in range(2):
                        pe.transpose(pt[b][:, 2 * c + h, :], r[p][:, 2 * g + h, c * P:(c + 1) * P], k.ident[:],
                                     name=f"turned{b}")
                k.p.alias(f"r_turned{p}", f"turned{b}")
                act.wait(f"turned{b}", f"scores_a{p}", f"y_in{p}")
                act.act(wt[p][:, :, 2 * g:2 * g + 2, :], pt[b][:].rearrange("p (c h) t -> p c h t", c=2),
                        ACT.Square, name=f"w_out{b}")
                k.p.alias(f"weights{p}", f"w_out{b}")

        def result(p):
            pe.wait(f"weights{p}", "y_out")
            pe.products(py[:, 0:D], [(wt[p][:, c, h, :], k.to_out[:, h, c, :])
                                     for h in range(HH) for c in range(2)], name=f"y_in{p}")
            v.wait(f"y_in{p}")
            v.tt(lambda i: k.x[:, ds(2 * i + p, 1), :], lambda i: k.x[:, ds(2 * i + p, 1), :], py[:, 0:D],
                 ALU.add, name="y_out")

        k.p.loop(NT // 2)
        state(0)
        state(1)
        scores(0, 0)
        scores(1, 0)
        for step in range(3):
            for _ in zip(threshold(0), threshold(1)):
                pass
            for p in range(2):
                weights(p)
                if step < 2:
                    scores(p, step + 1)
                else:
                    result(p)
        k.p.end_loop()


def two_layer_kernel(nc, ins, out, only=None):
    with ExitStack() as ctx:
        k = Kernel(nc, ctx, ins, out)
        k.rec_q = nc.dram_tensor("rec_q", [B * H, REC, S], F32, kind="Internal").ap()
        k.rec_k = nc.dram_tensor("rec_k", [B * H, REC, S], F32, kind="Internal").ap()
        k.x = k.sb("x", [P, NT, D])
        constants(k)
        blend = k.sb("blend", [P, 2, 4, 2])
        k.p.barrier()
        with scope(k):
            k.vals = k.sb("vals", [P, NT, H, 32])
            k.heads = k.sb("heads", [P, B * H, QT, HD])
            with scope(k):
                k.xh, k.xl = k.sb("xh", [P, DC, T], F32R), k.sb("xl", [P, DC, T], F32R)
                first_norm(k)
                blend_weights(k, blend)
                queries_and_keys(k)
                swiglu(k)
            attention(k, ["gsa", "std"], [blend[:, 0], blend[:, 1]])
            output_projection(k, "wo0", k.x)
        k.h = k.sb("h", [P, NT, D])
        k.hop_mean, k.hop_scale, k.rms = k.sb("hop_mean", [P, NT]), k.sb("hop_scale", [P, NT]), k.sb("rms", [P, NT])
        second_norm(k)
        with scope(k):
            k.to_scores, k.again, k.to_out = (k.sb(n, [P, HH, 2, NM]) for n in ("to_scores", "again", "to_out"))
            hopfield_weights(k)
            hopfield(k)
        with scope(k):
            k.vals = k.sb("vals", [P, NT, H, 32])
            k.heads = k.sb("heads", [P, B * H, QT, HD])
            with scope(k):
                k.xh, k.xl = k.sb("xh", [P, DC, T], F32R), k.sb("xl", [P, DC, T], F32R)
                latent_projections(k)
            one = k.sb("one", [P, 4, 2])
            k.pool.memset(one[:], 1.0, name="one")
            k.pool.wait("one")
            attention(k, ["std"], [one[:]])
            output_projection(k, "lat_o", k.h)
        with scope(k):
            k.xh, k.xl = k.sb("xh", [P, DC, T], F32R), k.sb("xl", [P, DC, T], F32R)
            experts(k)
        k.sp.dma(out, k.x[:], k.dma_counter("result"), "result")
        k.p.barrier()
        block = ctx.enter_context(nc.Block())
        block.sync(lambda e: k.sp.play(e))
        block.scalar(lambda e: k.act.play(e))
        block.vector(lambda e: k.dve.play(e))
        block.gpsimd(lambda e: k.pool.play(e))
        block.tensor(lambda e: k.pe.play(e))


def blend_weights(k, blend):
    with scope(k):
        sc, b = k.sb("sc", [P, 5]), k.sb("b", [P, 2])
        k.load((sc[:], "splat_scalars"))
        k.p.barrier()
        v = k.dve
        k.act.act(b[:, 0:1], sc[:, 4:5], ACT.Exp, scale=-1.0, name="b")
        v.wait("b")
        for op, s1, o2, s2 in ((ALU.add, 1.0, None, None), (None,) * 4, (ALU.mult, 0.15, ALU.min, 0.03)):
            if op is None:
                v.recip(b[:, 0:1], b[:, 0:1], name="v")
            elif o2 is None:
                v.ts(b[:, 0:1], b[:, 0:1], s1, op, name="v")
            else:
                v.ts(b[:, 0:1], b[:, 0:1], s1, op, s2, o2, name="v")
            v.wait("v")
        v.ts(b[:, 1:2], b[:, 0:1], -1.0, ALU.mult, 1.0, ALU.add, name="v")
        v.wait("v")
        for n in range(2):
            v.copy(blend[:, n], b[:, n:n + 1].unsqueeze(2).to_broadcast([P, 4, 2]), name="v")




def layout(a):
    f = {n: np.asarray(v, np.float32) if np.ndim(v) == 0 else np.asarray(v) for n, v in a.items()}

    def rows(w):
        return w.reshape(-1, P, w.shape[1]).transpose(1, 0, 2)

    def spread(v, n=P):
        return np.broadcast_to(np.asarray(v).reshape(1, -1), (n, np.asarray(v).size))

    def col(v):
        return v.reshape(-1, P).T

    o = {}
    x = rows(f["L0_attn_hidden_states"].reshape(T, D))
    o["x_a"], o["x_b"] = x[:, :NT // 2], x[:, NT // 2:]
    o["wqk0"] = rows(np.concatenate([f["L0_attn_Wq"].T, f["L0_attn_Wk"].T], 1))
    o["wv0"], o["wo0"] = rows(f["L0_attn_Wv"].T), rows(f["L0_attn_Wo"].T)
    pos, dirs = f["L0_attn_splat_positions"], f["L0_attn_splat_directions"]
    for name, t in (("splat_pos", pos), ("splat_dir", dirs), ("neg_half", None)):
        m = np.zeros((D, H * NS), np.float32)
        for h in range(H):
            m[h * HD:(h + 1) * HD, h * NS:(h + 1) * NS] = -0.5 if t is None else t[h].T
        o[name] = rows(m)
    o["pos_rows"], o["dir_rows"] = pos.reshape(P, HD), dirs.reshape(P, HD)
    o["splat_scalars"] = np.concatenate(
        [f["L0_attn_splat_log_scales"].reshape(P, 1), f["L0_attn_splat_log_amplitudes"].reshape(P, 1)]
        + [spread(f["L0_attn_" + n]) for n in ("directional_strength", "position_sensitivity", "gsa_strength")], 1)
    o["gate_w"], o["up_w"], o["down_w"] = (rows(f[f"L0_ffn_{n}_w"]).reshape(P, -1) for n in ("gate", "up", "down"))
    o["gate_s"], o["up_s"] = col(f["L0_ffn_gate_scale"]), col(f["L0_ffn_up_scale"])
    o["down_s"] = spread(f["L0_ffn_down_scale"])
    o["memory"] = rows(f["L1_attn_memory"])
    o["hop_q"] = rows(f["L1_attn_Wq"])
    for n, w in (("hop_k", "Wk"), ("hop_v", "Wv")):
        o[n] = f["L1_attn_" + w].T.reshape(P, HH, P)
    o["hop_o"] = rows(f["L1_attn_Wo"].T)
    o["g_mem"], o["b_mem"] = col(f["L1_attn_g_mem"]), col(f["L1_attn_b_mem"])
    o["g_state"], o["b_state"] = col(f["L1_attn_g_state"]), col(f["L1_attn_b_state"])
    o["log_beta"] = spread(f["L1_attn_log_beta"])
    g = {n[7:]: v for n, v in f.items() if n.startswith("L1_ffn_")}
    R, LAT = HD // 2, D // 4
    o["ln1_w"], o["ln2_w"] = col(g["ln1_w"]), col(g["ln2_w"])
    o["lat_down"] = rows(np.concatenate([g["kv_d_w"], g["q_d_w"]], 1))

    def heads(w, plain):
        m = np.zeros((w.shape[0], H, HD), np.float32)
        m[:, :, (0 if plain else R):(R if plain else HD)] = w.reshape(-1, H, R)
        return m.reshape(-1, D)

    def swapped(w):
        return w.reshape(-1, H, 2, R // 2)[:, :, ::-1].reshape(-1, H * R)

    qa = np.zeros((w := P, H, HD), np.float32)
    qa[LAT:, :, :R], qa[LAT:, :, R:] = g["q_u_w"].reshape(-1, H, R), g["rope_q_w"].reshape(-1, H, R)
    o["lat_qa"] = qa.reshape(P, D)
    o["lat_qb"] = np.concatenate([np.zeros((LAT, D), np.float32), heads(swapped(g["rope_q_w"]), False)])
    o["lat_kd"] = np.concatenate([heads(g["k_u_w"], True), np.zeros((LAT, D), np.float32)])
    o["lat_ka"], o["lat_kb"] = rows(heads(g["rope_k_w"], False)), rows(heads(swapped(g["rope_k_w"]), False))
    o["lat_v"] = np.concatenate([g["v_u_w"], np.zeros((LAT, D), np.float32)])
    o["lat_o"] = rows(g["o_w"])
    freq = (1.0 / np.float32(10000.0) ** (np.arange(0, R, 2, dtype=np.float32) / np.float32(R))).astype(np.float32)
    ang = np.outer(np.arange(S, dtype=np.float32), freq).astype(np.float32)
    ang = np.concatenate([ang, ang], 1)
    cos, sin = np.ones((HD, S), np.float32), np.zeros((HD, S), np.float32)
    cos[R:] = np.cos(ang).T
    sin[R:] = np.sin(ang).T
    sin[R:R + R // 2] *= -1
    o["rope_cos"], o["rope_sin"] = np.tile(cos, (8, B)), np.tile(sin, (8, B))
    for n in ("gate", "up"):
        w = np.concatenate([g["sh_" + n][None], g["r_" + n]])
        o["moe_" + n] = w.reshape(NE, DC, P, P).transpose(2, 1, 0, 3).reshape(P, DC, NE * P)
    o["moe_down"] = np.concatenate([g["sh_down"][None], g["r_down"]]).transpose(1, 0, 2)
    o["router_w"] = rows(np.concatenate([g["router_w"], np.zeros((D, 64 - NR), np.float32)], 1))
    o["router_b"] = spread(g["router_b"])
    return {n: np.ascontiguousarray(v) for n, v in o.items()}


def kernel(**inputs):
    import concourse.bacc as bacc
    from concourse.bass_utils import run_bass_kernel_spmd

    nc = bacc.Bacc("TRN2", target_bir_lowering=False, num_devices=1)
    arrays = layout(inputs)
    ins = {n: nc.dram_tensor("in_" + n, a.shape, mybir.dt.from_np(a.dtype), kind="ExternalInput").ap()
           for n, a in arrays.items()}
    out = nc.dram_tensor("out", (P, NT, D), F32, kind="ExternalOutput").ap()
    two_layer_kernel(nc, ins, out)
    r = run_bass_kernel_spmd(nc, [{"in_" + n: a for n, a in arrays.items()}], core_ids=[0])
    return np.ascontiguousarray(r.results[0]["out"].transpose(1, 0, 2).reshape(B, S, D))
```

```python
from contextlib import ExitStack, contextmanager

import numpy as np
import concourse.bass as bass
from concourse import mybir

F32 = mybir.dt.float32
F32R = mybir.dt.float32r
BF16 = mybir.dt.bfloat16
U32 = mybir.dt.uint32
ALU = mybir.AluOpType
ACT = mybir.ActivationFunctionType
X_AXIS = mybir.AxisListType.X
FUNCTION = type(lambda: 0)
ds = bass.ds

START = 2048


class Counter:

    def __init__(self, sem, step):
        self.sem, self.step, self.per_stage = sem, step, {}


class Program:

    def __init__(self):
        self.stages, self.lines, self.counters, self.marks = [], [], [], {}
        self.stage()

    def stage(self, trips=1):
        self.stages.append(trips)
        self.now = len(self.stages) - 1
        self.marks = {}
        self.pending = []

    def loop(self, trips):
        self.barrier()
        self.stage(trips)

    def end_loop(self):
        self.stage()
        self.barrier()

    def barrier(self):
        if self.stages[self.now] != 1:
            raise ValueError("no barrier inside a loop")
        now = self.now
        at = [(c, c.per_stage.get(now, 0)) for c in self.counters]
        for line in self.lines:
            for c, local in at:
                line.queue.append((now, {"at": (c, local), "lag": 0}))

    def mark(self, name, where):
        self.marks[name] = where
        for waited, found in self.pending:
            if waited == name:
                found["at"] = where

    def alias(self, name, other):
        self.mark(name, self.marks[other])

    def value(self, counter, local, now, lag):
        base = START + sum(self.stages[s] * counter.per_stage.get(s, 0) for s in range(now))
        return base + local - lag * counter.per_stage.get(now, 0)


class Line:

    def __init__(self, program, sem):
        self.program, self.counter, self.queue = program, Counter(sem, 1), []
        program.lines.append(self)
        program.counters.append(self.counter)

    def wait(self, *names):
        program = self.program
        for name in names:
            if name in program.marks:
                counter, local = program.marks[name]
                self.queue.append((program.now, {"at": (counter, local), "lag": 0}))
            elif program.stages[program.now] != 1:
                found = {"lag": 1}
                program.pending.append((name, found))
                self.queue.append((program.now, found))

    def op(self, emit, name=None, counter=None):
        program = self.program
        if name is None and counter is None:
            self.queue.append((program.now, emit))
            return
        c = counter or self.counter
        c.per_stage[program.now] = c.per_stage.get(program.now, 0) + c.step
        self.queue.append((program.now, lambda engine, i: emit(engine, i).then_inc(c.sem, c.step)))
        if name is not None:
            program.mark(name, (c, c.per_stage[program.now]))

    def starts(self):
        return [self.counter]

    def play(self, engine):
        program = self.program
        assert all(n <= START for c in program.counters for n in c.per_stage.values())
        for counter in self.starts():
            engine.sem_inc(counter.sem, START)
        for s, trips in enumerate(program.stages):
            body = [entry for stage, entry in self.queue if stage == s]
            if body and trips == 1:
                self.play_body(engine, body, s, 0)
            elif body:
                with engine.Fori(0, trips) as i:
                    self.play_body(engine, body, s, i)

    def play_body(self, engine, body, now, i):
        program, wanted, reached = self.program, {}, {}
        for entry in body + [None]:
            if type(entry) is dict:
                if "at" in entry:
                    counter, local = entry["at"]
                    value = program.value(counter, local, now, entry["lag"])
                    wanted[counter] = max(value, wanted.get(counter, 0))
                continue
            for counter, value in wanted.items():
                per = 0 if program.stages[now] == 1 else counter.per_stage.get(now, 0)
                if value > reached.get(counter, 0 if per else START):
                    reached[counter] = value
                    engine.wait_ge(counter.sem, i * per + value if per else value)
            wanted = {}
            if entry:
                entry(engine, i)


def at(x, i):
    return x(i) if type(x) is FUNCTION else x


class Tensor(Line):
    def mm(self, out, lhsT, rhs, start=True, stop=True, name=None):
        self.op(lambda e, i: e.matmul(at(out, i), at(lhsT, i), at(rhs, i), start=start, stop=stop), name)

    def transpose(self, out, in_, identity, name=None):
        self.op(lambda e, i: e.transpose(at(out, i), at(in_, i), identity), name)

    def products(self, out, pairs, name=None):
        for n, (lhsT, rhs) in enumerate(pairs):
            last = n == len(pairs) - 1
            self.mm(out, lhsT, rhs, n == 0, last, name if last else None)


class Scalar(Line):
    def act(self, out, in_, func=ACT.Copy, bias=0.0, scale=1.0, accum=None, name=None):
        self.op(lambda e, i: e.activation(at(out, i), at(in_, i), func, bias=at(bias, i), scale=at(scale, i),
                                          accum_out=accum), name)

    def dma(self, out, in_, counter, name):
        self.op(lambda e, i: e.dma_start(at(out, i), at(in_, i)), name, counter)


class Vector(Line):
    def tt(self, out, a, b, op, name=None):
        self.op(lambda e, i: e.tensor_tensor(at(out, i), at(a, i), at(b, i), op), name)

    def ts(self, out, a, s1, op0, s2=None, op1=ALU.bypass, accum=None, name=None):
        self.op(lambda e, i: e.tensor_scalar(at(out, i), at(a, i), at(s1, i), at(s2, i), op0, op1, accum_out=accum), name)

    def stt(self, out, a, s, b, op0, op1, name=None):
        self.op(lambda e, i: e.scalar_tensor_tensor(at(out, i), at(a, i), at(s, i), at(b, i), op0, op1), name)

    def copy(self, out, a, name=None):
        self.op(lambda e, i: e.tensor_copy(at(out, i), at(a, i)), name)

    def recip(self, out, a, name=None):
        self.op(lambda e, i: e.reciprocal(at(out, i), at(a, i)), name)

    def reduce(self, out, a, op, negate=None, name=None):
        self.op(lambda e, i: e.tensor_reduce(at(out, i), at(a, i), X_AXIS, op, negate=negate), name)

    def memset(self, out, v, name=None):
        self.op(lambda e, i: e.memset(out, v), name)


class Sync(Line):
    def starts(self):
        return [self.counter] + [c for c in self.program.counters if c.step == 16]

    def dma(self, out, in_, counter, name):
        self.op(lambda e, i: e.dma_start(at(out, i), at(in_, i)), name, counter)


def f32(x):
    return (lambda i: x(i).bitcast(F32)) if type(x) is FUNCTION else x.bitcast(F32)


P = 128
B, S, D = 2, 1024, 256
T = B * S
NT = T // P
DC = D // P
NB = T // 512
H, HD, NS = 16, 16, 8
QT = S // P
F0 = 768
FC = F0 // P
HH, NM = 8, 256
MC = NM // P
NE, NR = 8, 7
EPS = 1e-5
BIG = -3.0e38
NEWTON = 5

REC = 64
KROW = 96
STACK = KROW + 1


class Kernel:

    def __init__(self, nc, ctx, ins, out):
        self.nc, self.ctx, self.ins, self.out = nc, ctx, ins, out
        self.p = p = Program()
        def sem(n):
            return ctx.enter_context(nc.semaphore(n))
        self.pe, self.act, self.dve = Tensor(p, sem("pe")), Scalar(p, sem("act")), Vector(p, sem("dve"))
        self.pool, self.sp = Vector(p, sem("pool")), Sync(p, sem("sp"))
        self.dma_sems = {}
        self.scopes = [ctx]
        self.n = 0

    def dma_counter(self, name):
        if name not in self.dma_sems:
            c = Counter(self.ctx.enter_context(self.nc.semaphore("dma_" + name)), 16)
            self.p.counters.append(c)
            self.dma_sems[name] = c
        return self.dma_sems[name]

    def sb(self, name, shape, dt=F32):
        self.n += 1
        return self.scopes[-1].enter_context(self.nc.sbuf_tensor(f"{name}_{self.n}", shape, dt))

    def ps(self, name, shape, dt=F32):
        self.n += 1
        n = int(np.prod(shape[1:]))
        t = self.scopes[-1].enter_context(self.nc.psum_tensor(f"{name}_{self.n}", [P, -(-n // 512) * 512], dt))
        dims = "abcd"[:len(shape) - 1]
        return t[:, 0:n].rearrange(f"p ({' '.join(dims)}) -> p {' '.join(dims)}",
                                   **dict(zip(dims, shape[1:]))) if len(dims) > 1 else t[:, 0:n]

    def load(self, *pairs):
        for tile, name in pairs:
            src = self.ins[name]
            self.sp.dma(tile, src, self.dma_counter("weights"), "load_" + name)

    def split(self, hi, lo, src, tag):
        self.act.act(hi, src, name=f"{tag}_hi")
        self.dve.wait(f"{tag}_hi")
        self.dve.tt(lo, src, f32(hi), ALU.subtract, name=f"{tag}_lo")


@contextmanager
def scope(k):
    with ExitStack() as s:
        k.scopes.append(s)
        yield
        k.p.barrier()
        k.scopes.pop()


def constants(k):
    k.ident = k.sb("ident", [P, P])
    k.identb = k.sb("identb", [P, P], BF16)
    k.mask_q = k.sb("mask_q", [P, P], BF16)
    k.mask_k = k.sb("mask_k", [P, P], BF16)
    k.strips = k.sb("strips", [P, 32])
    k.eps = k.sb("eps", [P, 1])
    pool = k.pool
    for n, t in enumerate((k.ident, k.identb, k.mask_q, k.mask_k, k.strips)):
        pool.memset(t[:], 0.0, name="cleared")
    pool.memset(k.eps[:], EPS, name="cleared")
    pool.wait("cleared")

    def diagonal(t, cmp, fill, base, step, mult):
        pool.op(lambda e, i: e.affine_select(out=t, in_=t, compare_op=cmp, fill=fill, base=base,
                                             pattern=[[step, t.shape[1]]], channel_multiplier=mult), "made")
    diagonal(k.ident[:], ALU.not_equal, 1.0, 0, -1, 1)
    diagonal(k.identb[:], ALU.not_equal, 1.0, 0, -1, 1)
    diagonal(k.mask_q[:], ALU.is_ge, BIG, 0, -1, 1)
    diagonal(k.mask_k[:], ALU.is_ge, BIG, 0, 1, -1)
    for c in range(4):
        diagonal(k.strips[:], ALU.not_equal, 1.0, -32 * c, -1, 1)
        pool.wait("made")


def moments(k, x, tag, n=NT, d=D):
    st = k.sb("bn", [P, n, 6])
    mean, var, half = k.sb("mean", [P, n]), k.sb("var", [P, n]), k.sb("half", [P, n])
    v = k.dve
    for t in range(n):
        v.op(lambda e, i, t=t: e.bn_stats(st[:, t, :], x[:, t, :]), "v")
    v.wait("v")
    v.tt(mean[:], st[:, :, 1], st[:, :, 4], ALU.add, name="v")
    v.tt(half[:], st[:, :, 1], st[:, :, 4], ALU.subtract, name="v")
    v.tt(var[:], st[:, :, 2], st[:, :, 5], ALU.add, name="v")
    v.wait("v")
    v.ts(mean[:], mean[:], 0.5, ALU.mult, name="v")
    v.tt(half[:], half[:], half[:], ALU.mult, name="v")
    v.wait("v")
    v.ts(half[:], half[:], 0.25, ALU.mult, name="v")
    v.wait("v")
    v.stt(var[:], var[:], 1.0 / d, half[:], ALU.mult, ALU.add, name="v")
    v.wait("v")
    return mean, var


def inverse_root(k, var, tag):
    k.act.wait("v")
    k.act.act(var[:], var[:], ACT.Sqrt, bias=k.eps[:], name=f"root_{tag}")
    k.dve.wait(f"root_{tag}")
    k.dve.recip(var[:], var[:], name="v")
    k.dve.wait("v")
    return var


def first_norm(k):
    vals = k.vals
    with scope(k):
        wv, wvh, wvl = k.sb("wv", [P, DC, D]), k.sb("wvh", [P, DC, D], F32R), k.sb("wvl", [P, DC, D], F32R)
        k.load((k.x[:, 0:NT // 2], "x_a"), (k.x[:, NT // 2:], "x_b"), (wv[:], "wv0"))
        k.p.barrier()
        k.split(wvh[:], wvl[:], wv[:], "wv")
        mean, var = moments(k, k.x, "ln0")
        inverse_root(k, var, "ln0")
        k.pool.memset(vals[:], 0.0, name="vals0")
        k.pool.wait("vals0")
        k.pool.memset(vals[:, :, :, HD:HD + 1], 1.0, name="vals1")
        xn = [k.sb("xn", [P, D]) for _ in range(2)]
        th = [k.sb("th", [P, DC, P], F32R) for _ in range(2)]
        tl = [k.sb("tl", [P, DC, P], F32R) for _ in range(2)]
        pt = [k.ps("pt", [P, DC, P]) for _ in range(2)]
        pv = [k.ps("pv", [P, D]) for _ in range(2)]
        k.p.loop(NT // 2)
        for p in range(2):
            def tile(i, p=p):
                return 2 * i + p
            k.dve.wait(f"turned{p}")
            k.dve.ts(xn[p][:], lambda i, p=p: k.x[:, ds(2 * i + p, 1), :],
                     lambda i, p=p: mean[:, ds(2 * i + p, 1)], ALU.subtract,
                     lambda i, p=p: var[:, ds(2 * i + p, 1)], ALU.mult, name=f"xn{p}")
            transposed_tile(k, p, xn, pt, th, tl)
            k.pe.wait(f"v_out{p}", f"th{p}", f"tl{p}")
            k.pe.products(pv[p][:], [(a[:, c, :], w[:, c, :]) for c in range(DC)
                                     for a, w in ((th[p], wvh), (th[p], wvl), (tl[p], wvh))], name=f"v_in{p}")
            k.act.wait(f"v_in{p}")
            k.act.act(lambda i, p=p: vals[:, ds(2 * i + p, 1), :, 0:HD],
                      pv[p][:].rearrange("p (o h d) -> p o h d", o=1, h=H), name=f"v_out{p}")
        k.p.end_loop()


def transposed_tile(k, p, xn, pt, th, tl):
    xh, xl = k.xh, k.xl
    k.pe.wait(f"xn{p}", f"th{p}", f"tl{p}")
    for c in range(DC):
        k.pe.transpose(pt[p][:, c, :], xn[p][:, c * P:(c + 1) * P], k.ident[:],
                       name=f"turned{p}" if c == DC - 1 else None)
    k.act.wait(f"turned{p}", f"copied{p}", f"v_in{p}")
    k.dve.wait(f"copied{p}", f"v_in{p}")
    k.act.act(th[p][:], pt[p][:], name=f"th{p}")
    k.dve.wait(f"th{p}")
    k.dve.tt(tl[p][:], pt[p][:], f32(th[p][:]), ALU.subtract, name=f"tl{p}")
    k.pool.wait(f"th{p}", f"tl{p}")
    k.pool.copy(lambda i, p=p: xh[:, :, ds((2 * i + p) * P, P)], f32(th[p][:]), name=f"copied{p}")
    k.pool.copy(lambda i, p=p: xl[:, :, ds((2 * i + p) * P, P)], f32(tl[p][:]), name=f"copied{p}")


def three(wh, wl, xh, xl, chunks=DC):
    return [(a(c), b(c)) for c in range(chunks) for a, b in ((wh, xh), (wl, xh), (wh, xl))]


def queries_and_keys(k):
    xh, xl = k.xh, k.xl
    with scope(k):
        w, wh, wl = (k.sb(n, [P, DC, 2 * D], t) for n, t in (("w", F32), ("wh", F32R), ("wl", F32R)))
        pos, dirs, half = (k.sb(n, [P, DC, P]) for n in ("pos", "dirs", "half"))
        ph, dh = k.sb("ph", [P, HD]), k.sb("dh", [P, HD])
        sc = k.sb("sc", [P, 5])
        k.load((w[:], "wqk0"), (pos[:], "splat_pos"), (dirs[:], "splat_dir"), (half[:], "neg_half"),
               (ph[:], "pos_rows"), (dh[:], "dir_rows"), (sc[:], "splat_scalars"))
        k.p.barrier()
        k.split(wh[:], wl[:], w[:], "wqk")
        tmp, q = k.sb("tmp", [P, HD]), k.sb("cols", [P, 10])
        inv_s2, b_gauss, inv_n, b_dir, amp = (q[:, n:n + 1] for n in range(5))
        pp, dd, pd = (q[:, n:n + 1] for n in range(5, 8))
        v = k.dve
        k.act.act(inv_s2, sc[:, 0:1], ACT.Exp, scale=-2.0, name="splat_exp")
        k.act.act(amp, sc[:, 1:2], ACT.Exp, name="splat_exp")
        for a, b, o in ((ph, ph, pp), (dh, dh, dd), (ph, dh, pd)):
            v.tt(tmp[:], a[:], b[:], ALU.mult, name="v")
            v.wait("v")
            v.reduce(o, tmp[:], ALU.add, name="v")
            v.wait("v")
        k.act.wait("v")
        k.act.act(dd, dd, ACT.Sqrt, name="splat_norm")
        v.wait("splat_norm", "splat_exp")
        v.ts(dd, dd, 1e-8, ALU.add, name="v")
        v.wait("v")
        v.recip(inv_n, dd, name="v")
        v.stt(b_gauss, pp, -0.5, inv_s2, ALU.mult, ALU.mult, name="v")
        v.wait("v")
        v.stt(b_dir, pd, -1.0, inv_n, ALU.mult, ALU.mult, name="v")
        v.tt(amp, amp, sc[:, 3:4], ALU.mult, name="v")
        v.wait("v")
        strength = sc[:, 2:3]
        dims = [[k.ps("dims", [P, 512]) for _ in range(DC)] for _ in range(2)]
        gp, dp = [k.ps("gp", [P, 512]) for _ in range(2)], [k.ps("dp", [P, 512]) for _ in range(2)]
        raw, sq = ([[k.sb(n, [P, 512]) for _ in range(DC)] for _ in range(2)] for n in ("raw", "sq"))
        hi, lo = ([[k.sb(n, [P, 512], F32R) for _ in range(DC)] for _ in range(2)] for n in ("hi", "lo"))
        g, th, f1, f2 = ([k.sb(n, [P, 512]) for _ in range(2)] for n in ("g", "t", "f1", "f2"))
        fs = [[k.sb("fs", [P, 512], F32R) for _ in range(4)] for _ in range(2)]
        k.p.loop(NB)
        for s, scratch in ((0, k.rec_q), (1, k.rec_k)):
            tag, scale = "qk"[s], (HD ** -0.5, 1.0)[s]
            for c in range(DC):
                n = f"{tag}{c}"
                k.pe.wait(f"{n}_sq")
                k.pe.products(dims[s][c][:], three(
                    lambda a, s=s, c=c: wh[:, a, s * D + c * P:s * D + (c + 1) * P],
                    lambda a, s=s, c=c: wl[:, a, s * D + c * P:s * D + (c + 1) * P],
                    lambda a: lambda i, a=a: xh[:, a, ds(i * 512, 512)],
                    lambda a: lambda i, a=a: xl[:, a, ds(i * 512, 512)]), name=f"{n}_dims")
                k.act.wait(f"{n}_dims", f"{tag}_gauss_in", f"{tag}_dir_in", f"{n}_lo")
                k.act.act(raw[s][c][:], dims[s][c][:], name=f"{n}_raw")
                k.act.act(sq[s][c][:], dims[s][c][:], ACT.Square, name=f"{n}_sq")
                v.wait(f"{n}_raw", f"{n}_sent")
                v.ts(hi[s][c][:], raw[s][c][:], scale, ALU.mult, name=f"{n}_hi")
                v.wait(f"{n}_hi")
                v.stt(lo[s][c][:], raw[s][c][:], scale, f32(hi[s][c][:]), ALU.mult, ALU.subtract, name=f"{n}_lo")
                k.sp.wait(f"{n}_lo")
                for r, t in ((0, hi), (HD, lo)):
                    k.sp.dma(lambda i, c=c, r=r, scratch=scratch: scratch[
                        ds((i // 2) * H + c * 8, 8), r:r + HD, ds((i % 2) * 512, 512)], f32(t[s][c][:]),
                        k.dma_counter(f"{n}_sent"), f"{n}_sent")
            k.pe.wait(f"{tag}_g", f"{tag}0_sq", f"{tag}1_sq", f"{tag}0_raw", f"{tag}1_raw")
            k.pe.products(gp[s][:], [(half[:, c, :], sq[s][c][:]) for c in range(DC)]
                          + [(pos[:, c, :], raw[s][c][:]) for c in range(DC)], name=f"{tag}_gauss_in")
            k.pe.wait(f"{tag}_t")
            k.pe.products(dp[s][:], [(dirs[:, c, :], raw[s][c][:]) for c in range(DC)], name=f"{tag}_dir_in")
            k.act.wait(f"{tag}_gauss_in", f"{tag}_f1", f"{tag}_f2")
            k.act.act(g[s][:], gp[s][:], ACT.Exp, bias=b_gauss, scale=inv_s2, name=f"{tag}_g")
            k.act.wait(f"{tag}_dir_in")
            k.act.act(th[s][:], dp[s][:], ACT.Tanh, bias=b_dir, scale=inv_n, name=f"{tag}_t")
            v.wait(f"{tag}_g", f"{tag}_t", f"{tag}_sent", f"{tag}_split")
            if s == 0:
                v.ts(f1[s][:], g[s][:], amp, ALU.mult, name=f"{tag}_f1")
                v.wait(f"{tag}_f1")
                v.stt(f2[s][:], f1[s][:], strength, th[s][:], ALU.mult, ALU.mult, name=f"{tag}_f2")
            else:
                v.copy(f1[s][:], g[s][:], name=f"{tag}_f1")
                v.tt(f2[s][:], g[s][:], th[s][:], ALU.mult, name=f"{tag}_f2")
            v.wait(f"{tag}_f2")
            v.copy(fs[s][0][:], f1[s][:], name=f"{tag}_fh")
            v.copy(fs[s][1][:], f2[s][:], name=f"{tag}_fh")
            v.wait(f"{tag}_fh")
            v.tt(fs[s][2][:], f1[s][:], f32(fs[s][0][:]), ALU.subtract, name=f"{tag}_split")
            v.tt(fs[s][3][:], f2[s][:], f32(fs[s][1][:]), ALU.subtract, name=f"{tag}_split")
            k.sp.wait(f"{tag}_split")
            for r in range(4):
                k.sp.dma(lambda i, r=r, scratch=scratch: scratch[
                    ds((i // 2) * H, H), 2 * HD + r * NS:2 * HD + (r + 1) * NS, ds((i % 2) * 512, 512)],
                    f32(fs[s][r][:]), k.dma_counter(f"{tag}_sent"), f"{tag}_sent")
        k.p.end_loop()


def attention(k, kinds, blend):
    vals, heads = k.vals, k.heads
    nk = len(kinds)
    with scope(k):
        qs = [{kind: k.sb("q_" + kind, [P, S], F32R) for kind in kinds} for _ in range(3)]
        ks = [k.sb("keys", [P, S], F32R) for _ in range(3)]
        vb = [k.sb("values", [P, QT, 32]) for _ in range(3)]
        negmax = [{kind: k.sb("negmax", [P, 2, QT]) for kind in kinds} for _ in range(3)]
        low = [k.sb("p_low", [P, 4, 512]) for _ in range(4 - nk)]
        high = [k.sb("p_high", [P, 4, 512]) for _ in range(2)]
        strip = [k.sb("strip", [P, 512]) for _ in range(2 * nk)]
        rows = k.sb("rows", [P, 512])
        rec, tmp = k.sb("rec", [P, 4, 2 * nk]), k.sb("tmp", [P, 4, 2 * nk, HD])
        wts = k.sb("wts", [P, 4, 2 * nk])
        px = k.ps("px", [P, 2, 512])
        pss = k.ps("pss", [P, 4, 512])
        po, pr = k.ps("po", [P, 512]), k.ps("pr", [P, 512])
        pool, pe, act, v, sp = k.pool, k.pe, k.act, k.dve, k.sp
        for p in range(3):
            v.memset(f32(ks[p][:]), 0.0, name="clear_keys")
            for kind in kinds:
                v.memset(f32(qs[p][kind][:]), 0.0, name="clear_v")
        for t in low:
            v.memset(t[:], 0.0, name="clear_v")
        pool.memset(rows[:], 0.0, name="clear")
        pool.wait("clear_keys", "clear")
        for p in range(3):
            pool.memset(f32(ks[p][KROW:KROW + 1, :]), 1.0, name="clear")
        pool.wait("clear")
        for n in range(nk):
            pool.copy(wts[:, :, 2 * n:2 * n + 2], blend[n], name="clear")
        k.p.barrier()

        def load(u, p):
            def rec_of(t, a, b):
                return lambda i: t[ds(u(i), 1), a:b, :]
            sp.wait(f"used{p}")
            parts = []
            for kind in kinds:
                parts += [(qs[p][kind], 0, k.rec_q, 0, 32), (qs[p][kind], 32, k.rec_q, 0, 16)]
            parts += [(ks[p], 0, k.rec_k, 0, 16), (ks[p], 16, k.rec_k, 0, 32)]
            if "gsa" in kinds:
                parts += [(qs[p]["gsa"], 48, k.rec_q, 32, 64), (qs[p]["gsa"], 80, k.rec_q, 32, 48),
                          (ks[p], 48, k.rec_k, 32, 48), (ks[p], 64, k.rec_k, 32, 64)]
            for t, r, src, a, b in parts:
                sp.dma(f32(t[r:r + b - a, :]), rec_of(src, a, b), k.dma_counter(f"head{p}"), f"head{p}")
            pool.wait(f"used{p}")
            pool.copy(vb[p][:], lambda i: vals[:, ds((u(i) // H) * QT, QT), ds(u(i) % H, 1), :],
                      name=f"values{p}")

        def maxima(p):
            for kind in kinds:
                for t in range(QT):
                    width = (t + 1) * P
                    q = qs[p][kind][0:KROW, t * P:width]
                    for n, c in enumerate(range(0, width, 512)):
                        w, b = min(512, width - c), t % 2 if t < 4 else n
                        bank, diag = px[:, b, :], width - c <= 512
                        pe.wait(f"head{p}", f"x_read{b}")
                        pe.mm(bank[:, 0:w], q, ks[p][0:KROW, c:c + w], True, not diag,
                              name=None if diag else f"x{p}")
                        if diag:
                            pe.mm(bank[:, w - P:w], k.identb[:], k.mask_q[:], False, True, name=f"x{p}")
                        v.wait(f"x{p}", f"max_turned{p}")
                        v.reduce(negmax[p][kind][:, n, t:t + 1], bank[:, 0:w], ALU.max, negate=True,
                                 name=f"x_read{b}")
                        yield
                v.wait("x_read0", "x_read1")
                v.tt(negmax[p][kind][:, 0, 4:QT], negmax[p][kind][:, 0, 4:QT], negmax[p][kind][:, 1, 4:QT],
                     ALU.min, name=f"max_whole{p}")
                pe.wait(f"max_whole{p}")
                pe.wait("x_read0", "x_read1")
                for t in range(QT):
                    pe.mm(px[KROW:KROW + 1, t // 4, (t % 4) * P:(t % 4 + 1) * P],
                          negmax[p][kind][:, 0, t:t + 1], k.ident[:], name=f"max_turned{p}")
                act.wait(f"max_turned{p}")
                act.act(qs[p][kind][KROW:KROW + 1, :].rearrange("r (b w) -> r b w", b=2),
                        px[KROW:KROW + 1, :, :], name=f"max_row{p}")
                k.p.alias("x_read0", f"max_row{p}")
                k.p.alias("x_read1", f"max_row{p}")
                yield

        def weights(p, n, half, j, s):
            kind = kinds[n]
            pe.wait(f"exp{s % 2}", f"max_row{p}")
            spans = []
            for m in range(2):
                q0 = max(half * 512, (j + m) * P)
                w = (half + 1) * 512 - q0
                diag = (j + m) * P >= half * 512
                out = pss[:, 2 * (s % 2) + m, 512 - w:512]
                pe.mm(out, ks[p][0:STACK, (j + m) * P:(j + m + 1) * P], qs[p][kind][0:STACK, q0:q0 + w],
                      True, not diag, name=None if diag else f"scores{s % 2}")
                if diag:
                    pe.mm(pss[:, 2 * (s % 2) + m, 512 - w:512 - w + P], k.identb[:], k.mask_k[:],
                          False, True, name=f"scores{s % 2}")
                spans.append(w)
            buf, name = buffer(p, n, half, j)
            act.wait(f"scores{s % 2}", f"{name}_read")
            for m in ((slice(0, 2),) if spans[0] == spans[1] else (0, 1)):
                w = 512 if type(m) is slice else spans[m]
                bank = slice(2 * (s % 2), 2 * (s % 2) + 2) if type(m) is slice else 2 * (s % 2) + m
                tile = slice(j % 4, j % 4 + 2) if type(m) is slice else j % 4 + m
                act.act(buf[:, tile, 512 - w:512], pss[:, bank, 512 - w:512], ACT.Exp, name=f"exp{s % 2}")
                k.p.alias(f"{name}_made", f"exp{s % 2}")

        def buffer(p, n, half, j):
            turn = (p if nk == 1 else n) if half == 0 else j // 4
            return (low, high)[half][turn], f"{('low', 'high')[half]}{turn}"

        def values(p, n, half, j):
            buf, name = buffer(p, n, half, j)
            pe.wait(f"{name}_made", f"values{p}")
            if j == 0:
                pe.wait("po_read")
            for m in range(4):
                w = 512 if half == 0 or j == 0 else 512 - m * P
                pe.mm(po[32 * m:32 * m + 32, 512 - w:512], vb[p][:, j + m, :], buf[:, m, 512 - w:512],
                      j == 0, half == 0 or j > 0, name=f"{name}_read" if m == 3 else None)
            if j == 4 * half:
                v.wait(f"{name}_read", f"strip_read")
                v.copy(strip[2 * n + half][:], po[:], name="po_read")

        def finish(u):
            pe.wait("po_read", "out_read")
            for c in range(2 * nk):
                pe.mm(pr[32 * c:32 * c + 32, :], k.strips[:], strip[c][:], name="strip_read")
            rw = 64 * nk
            act.wait("strip_read", "rows_read")
            act.act(rows[0:rw, :], pr[0:rw, :], name="rows")
            yield
            pe.wait("rows")
            for t in range(4):
                pe.transpose(pr[:, t * P:(t + 1) * P], rows[:, t * P:(t + 1) * P], k.ident[:], name="rows_read")
            v.wait("rows_read", "tmp_read")
            ov = pr[:].rearrange("p (t m r) -> p t m r", t=4, m=4)[:, :, 0:2 * nk, :]
            v.recip(rec[:], ov[:, :, :, HD], name="rec")
            v.wait("rec")
            v.tt(rec[:], rec[:], wts[:], ALU.mult, name="rec")
            v.wait("rec")
            for t in range(4):
                v.tt(tmp[:, t], ov[:, t, :, 0:HD], rec[:, t].unsqueeze(2).to_broadcast([P, 2 * nk, HD]),
                     ALU.mult, name="out_read")
            pool.wait("out_read")
            for half in range(2):
                dst = lambda i, half=half: heads[:, ds(u(i), 1), half * 4:half * 4 + 4, :]
                if nk == 2:
                    pool.tt(dst, tmp[:, :, half, :], tmp[:, :, 2 + half, :], ALU.add, name="tmp_read")
                else:
                    pool.copy(dst, tmp[:, :, half, :], name="tmp_read")

        def run(gen):
            for _ in gen or ():
                pass

        def head(u, p, before=None, after=None, load_next=None):
            quads = [(n, half, j) for n in range(nk) for half in range(2) for j in range(0, 4 * (half + 1), 4)]
            slots, total = 0, (QT + 4 + 1) * nk
            other, ending, done = after, None, 0

            def slot():
                nonlocal slots, done
                slots += 1
                while other and done * (3 * len(quads)) < slots * total:
                    next(other, None)
                    done += 1

            for q, (n, half, j) in enumerate(quads):
                weights(p, n, half, j, 2 * q)
                slot()
                weights(p, n, half, j + 2, 2 * q + 1)
                slot()
                if q == 0 and before:
                    values(before[1], nk - 1, 1, 4)
                    k.p.alias(f"used{before[1]}", "high1_read")
                    if load_next:
                        load(*load_next)
                elif q:
                    if q == 1 and before:
                        ending = finish(before[0])
                        next(ending)
                    values(p, *quads[q - 1])
                    if ending and q == 2:
                        run(ending)
                elif load_next:
                    load(*load_next)
                slot()
            run(other)

        load(lambda i: 0, 0)
        load(lambda i: 1, 1)
        run(maxima(0))
        head(lambda i: 0, 0, None, maxima(1), (lambda i: 2, 2))
        k.p.loop((B * H - 2) // 3)
        for m in range(3):
            before = (lambda i, m=m: 3 * i + m, m)
            head(lambda i, m=m: 3 * i + m + 1, (m + 1) % 3, before, maxima((m + 2) % 3),
                 (lambda i, m=m: (3 * i + m + 3) % (B * H), m))
        k.p.end_loop()
        last = B * H - 1
        head(lambda i: last, last % 3, (lambda i: last - 1, (last - 1) % 3))
        values(last % 3, nk - 1, 1, 4)
        run(finish(lambda i: last))
        k.p.barrier()


def swiglu(k):
    xh, xl = k.xh, k.xl
    with scope(k):
        gw, uw = (k.sb(n, [P, DC, F0], F32R) for n in ("gw", "uw"))
        dw = k.sb("dw", [P, FC, D])
        gs, us, dsc = k.sb("gs", [P, FC]), k.sb("us", [P, FC]), k.sb("dsc", [P, D])
        with scope(k):
            raw = [k.sb("raw", [P, DC * F0]) for _ in range(3)]
            unit = k.sb("unit", [P, DC * F0])
            k.load((raw[0][:], "gate_w"), (raw[1][:], "up_w"), (raw[2][:], "down_w"), (gs[:], "gate_s"),
                   (us[:], "up_s"), (dsc[:], "down_s"))
            k.p.barrier()
            v = k.dve
            for w, out in zip(raw, (gw[:].rearrange("p c f -> p (c f)"), uw[:].rearrange("p c f -> p (c f)"),
                                    dw[:].rearrange("p c f -> p (c f)"))):
                v.wait("v")
                v.ts(unit[:].bitcast(U32), w[:].bitcast(U32), 0x7F800000, ALU.bitwise_and, name="v")
                v.wait("v")
                v.ts(unit[:], unit[:], 2.0 ** -6, ALU.max, 1.5 * 2.0 ** 20, ALU.mult, name="v")
                v.wait("v")
                v.tt(w[:], w[:], unit[:], ALU.add, name="v")
                v.wait("v")
                v.tt(w[:], w[:], unit[:], ALU.subtract, name="v")
                v.wait("v")
                v.stt(unit[:], w[:], -1.0, w[:], ALU.mult, ALU.max, name="v")
                v.wait("v")
                v.ts(unit[:], unit[:], 448.0, ALU.is_gt, 3.0e38, ALU.mult, name="v")
                v.wait("v")
                v.stt(out, unit[:], 3.0e38, w[:], ALU.mult, ALU.add, name="v")
        pg, pu = [k.ps("pg", [P, 512]) for _ in range(2)], [k.ps("pu", [P, 512]) for _ in range(2)]
        py = [k.ps("py", [P, D]) for _ in range(2)]
        sg = [k.sb("sg", [P, 512]) for _ in range(2)]
        fz = k.sb("fz", [P, FC, 512])
        y = [k.sb("y", [P, D]) for _ in range(2)]
        k.p.loop(NB)
        for f in range(FC):
            b = f % 2
            for w, out, n in ((gw, pg[b], "g"), (uw, pu[b], "u")):
                k.pe.wait(f"silu{b}" if n == "g" else f"fused{b}")
                k.pe.products(out[:], [(w[:, c, f * P:(f + 1) * P],
                                        lambda i, c=c, x=x: x[:, c, ds(i * 512, 512)])
                                       for c in range(DC) for x in (xh, xl)], name=f"{n}{b}")
            k.act.wait(f"g{b}", f"fused{b}")
            k.act.act(sg[b][:], pg[b][:], ACT.Silu, scale=gs[:, f:f + 1], name=f"silu{b}")
            k.dve.wait(f"silu{b}", f"u{b}", "down1", "down0")
            k.dve.stt(fz[:, f, :], pu[b][:], us[:, f:f + 1], sg[b][:], ALU.mult, ALU.mult, name=f"fused{b}")
        for t in range(4):
            b = t % 2
            k.pe.wait("fused0", "fused1", f"scaled{b}")
            k.pe.products(py[b][:], [(fz[:, f, t * P:(t + 1) * P], dw[:, f, :]) for f in range(FC)], name=f"down{b}")
            k.dve.wait(f"down{b}", f"added{b}")
            k.dve.tt(y[b][:], py[b][:], dsc[:], ALU.mult, name=f"scaled{b}")
            k.dve.wait(f"scaled{b}")
            k.dve.tt(lambda i, t=t: k.x[:, ds(4 * i + t, 1), :], lambda i, t=t: k.x[:, ds(4 * i + t, 1), :],
                     y[b][:], ALU.add, name=f"added{b}")
        k.p.end_loop()


def output_projection(k, weight, into):
    heads = k.heads
    with scope(k):
        w = k.sb("wo", [P, DC, D])
        k.load((w[:], weight))
        k.p.barrier()
        o = [k.sb("o", [P, D]) for _ in range(4)]
        ot = [k.sb("ot", [P, DC, P]) for _ in range(4)]
        pt, py = [k.ps("pt", [P, DC, P]) for _ in range(4)], [k.ps("py", [P, D]) for _ in range(4)]
        k.p.loop(NT // 4)
        for p in range(4):
            k.pool.wait(f"turned{p}")
            k.pool.copy(o[p][:].rearrange("p (h d) -> p h d", h=H),
                        lambda i, p=p: heads[:, ds(((4 * i + p) // QT) * H, H), ds((4 * i + p) % QT, 1), :],
                        name=f"o{p}")
            k.pe.wait(f"o{p}", f"ot{p}")
            for c in range(DC):
                k.pe.transpose(pt[p][:, c, :], o[p][:, c * P:(c + 1) * P], k.ident[:], name=f"turned{p}")
            k.act.wait(f"turned{p}", f"y{p}")
            k.act.act(ot[p][:], pt[p][:], name=f"ot{p}")
            k.pe.wait(f"ot{p}", f"added{p}")
            k.pe.products(py[p][:], [(ot[p][:, c, :], w[:, c, :]) for c in range(DC)], name=f"y{p}")
            k.dve.wait(f"y{p}")
            k.dve.tt(lambda i, p=p: into[:, ds(4 * i + p, 1), :], lambda i, p=p: into[:, ds(4 * i + p, 1), :],
                     py[p][:], ALU.add, name=f"added{p}")
        k.p.end_loop()


def normalised_transpose(k, src, scale_col, features):
    xh, xl = k.xh, k.xl
    xn = [k.sb("xn", [P, D]) for _ in range(4)]
    pt = [k.ps("pt", [P, DC, P]) for _ in range(4)]
    k.p.loop(NT // 4)
    for p in range(4):
        k.dve.wait(f"turned{p}")
        k.dve.ts(xn[p][:], lambda i, p=p: src[:, ds(4 * i + p, 1), :],
                 lambda i, p=p: scale_col[:, ds(4 * i + p, 1)], ALU.mult, name=f"xn{p}")
        k.pe.wait(f"xn{p}", f"tl{p}")
        for c in range(DC):
            k.pe.transpose(pt[p][:, c, :], xn[p][:, c * P:(c + 1) * P], k.ident[:],
                           name=f"turned{p}" if c == DC - 1 else None)
        k.act.wait(f"turned{p}")
        for c in range(DC):
            k.act.act(lambda i, p=p, c=c: xh[:, c, ds((4 * i + p) * P, P)], pt[p][:, c, :],
                      scale=features[:, c:c + 1], name=f"th{p}")
    for p in range(4):
        k.dve.wait(f"th{p}")
        for c in range(DC):
            k.dve.stt(lambda i, p=p, c=c: xl[:, c, ds((4 * i + p) * P, P)], pt[p][:, c, :], features[:, c:c + 1],
                      lambda i, p=p, c=c: f32(xh[:, c, ds((4 * i + p) * P, P)]),
                      ALU.mult, ALU.subtract, name=f"tl{p}")
    k.p.end_loop()


def second_norm(k):
    with scope(k):
        mean, var = moments(k, k.x, "ln1")
        inverse_root(k, var, "ln1")
        for t in range(NT):
            k.dve.ts(k.h[:, t, :], k.x[:, t, :], mean[:, t:t + 1], ALU.subtract, var[:, t:t + 1], ALU.mult, name="v")
        k.dve.wait("v")
        mean2, var2 = moments(k, k.h, "ln1b")
        k.dve.copy(k.hop_mean[:], mean2[:], name="v")
        k.dve.copy(k.hop_scale[:], var2[:], name="v")
        k.dve.tt(mean2[:], mean2[:], mean2[:], ALU.mult, name="v")
        k.dve.wait("v")
        k.dve.tt(k.rms[:], mean2[:], var2[:], ALU.add, name="v")
        k.dve.wait("v")
        inverse_root(k, k.hop_scale, "hop")
        inverse_root(k, k.rms, "rms")


def latent_projections(k):
    xh, xl, vals = k.xh, k.xl, k.vals
    with scope(k):
        names = (("wd", "lat_down", [P, DC, P]), ("qa", "lat_qa", [P, D]), ("qb", "lat_qb", [P, D]),
                 ("kd", "lat_kd", [P, D]), ("ka", "lat_ka", [P, DC, D]), ("kb", "lat_kb", [P, DC, D]),
                 ("vu", "lat_v", [P, D]))
        hi, lo = {}, {}
        raws = []
        for n, src, shape in names:
            hi[n], lo[n] = k.sb(n + "h", shape, F32R), k.sb(n + "l", shape, F32R)
        cos, sin, ln1 = k.sb("cos", [P, T]), k.sb("sin", [P, T]), k.sb("ln1", [P, DC])
        with scope(k):
            for n, src, shape in names:
                raws.append((n, k.sb(n, shape), src))
            k.load(*((r[:], src) for _, r, src in raws), (cos[:], "rope_cos"), (sin[:], "rope_sin"), (ln1[:], "ln1_w"))
            k.p.barrier()
            for n, r, _ in raws:
                k.split(hi[n][:], lo[n][:], r[:], n)
        with scope(k):
            normalised_transpose(k, k.h, k.rms, ln1)
        v = k.dve
        v.memset(vals[:], 0.0, name="vals0")
        v.wait("vals0")
        v.memset(vals[:, :, :, HD:HD + 1], 1.0, name="vals1")
        k.act.wait("vals1")
        dh, dl = k.sb("dh", [P, 512], F32R), k.sb("dl", [P, 512], F32R)
        pd = k.ps("pd", [P, 512])
        pa, pb = [k.ps("pa", [P, 512]) for _ in range(2)], [k.ps("pb", [P, 512]) for _ in range(2)]
        pv = [k.ps("pv", [P, D]) for _ in range(2)]
        ta, tb = [k.sb("ta", [P, 512]) for _ in range(2)], [k.sb("tb", [P, 512]) for _ in range(2)]
        th, tl = [k.sb("oh", [P, 512], F32R) for _ in range(2)], [k.sb("ol", [P, 512], F32R) for _ in range(2)]

        def xs(w, c0):
            return three(lambda a: hi[w][:, a, c0:c0 + P], lambda a: lo[w][:, a, c0:c0 + P],
                         lambda a: lambda i, a=a: xh[:, a, ds(i * 512, 512)],
                         lambda a: lambda i, a=a: xl[:, a, ds(i * 512, 512)])

        def lat(w, c0, n=P, t=None):
            a, b = hi[w][:, c0:c0 + n], lo[w][:, c0:c0 + n]
            if t is None:
                return [(a, dh[:]), (b, dh[:]), (a, dl[:])]
            c, d = dh[:, t * P:(t + 1) * P], dl[:, t * P:(t + 1) * P]
            return [(c, a), (c, b), (d, a)]

        k.p.loop(NB)
        k.pe.wait("dh", "dl")
        k.pe.products(pd[:], xs("wd", 0), name="down")
        k.act.wait("down", "b1", "v1")
        k.act.act(dh[:], pd[:], name="dh")
        v.wait("dh", "b1", "v1")
        v.tt(dl[:], pd[:], f32(dh[:]), ALU.subtract, name="dl")
        for n, (s, c) in enumerate(((0, 0), (0, 1), (1, 0), (1, 1))):
            b = n % 2
            scratch, scale = ((k.rec_q, HD ** -0.5), (k.rec_k, 1.0))[s]
            c0 = c * P
            k.pe.wait("dl", "dh", f"ta{b}")
            k.pe.products(pa[b][:], lat("qa", c0) if s == 0 else lat("kd", c0) + xs("ka", c0), name=f"a{b}")
            k.pe.wait(f"tb{b}")
            k.pe.products(pb[b][:], lat("qb", c0) if s == 0 else xs("kb", c0), name=f"b{b}")
            v.wait(f"a{b}", f"b{b}", f"sent{b}", f"tl{b}")
            v.tt(ta[b][:], pa[b][:], lambda i: cos[:, ds(i * 512, 512)], ALU.mult, name=f"ta{b}")
            v.tt(tb[b][:], pb[b][:], lambda i: sin[:, ds(i * 512, 512)], ALU.mult, name=f"tb{b}")
            v.wait(f"ta{b}", f"tb{b}")
            v.tt(ta[b][:], ta[b][:], tb[b][:], ALU.add, name=f"sum{b}")
            v.wait(f"sum{b}")
            v.ts(th[b][:], ta[b][:], scale, ALU.mult, name=f"th{b}")
            v.wait(f"th{b}")
            v.stt(tl[b][:], ta[b][:], scale, f32(th[b][:]), ALU.mult, ALU.subtract, name=f"tl{b}")
            k.sp.wait(f"tl{b}")
            for r, t in ((0, th), (HD, tl)):
                k.sp.dma(lambda i, c=c, r=r, scratch=scratch: scratch[
                    ds((i // 2) * H + c * 8, 8), r:r + HD, ds((i % 2) * 512, 512)], f32(t[b][:]),
                    k.dma_counter(f"lat{b}"), f"sent{b}")
        for t in range(4):
            b = t % 2
            k.pe.wait(f"v_out{b}")
            k.pe.products(pv[b][:], lat("vu", 0, D, t), name=f"v{b}")
            k.act.wait(f"v{b}")
            k.act.act(lambda i, t=t: vals[:, ds(4 * i + t, 1), :, 0:HD],
                      pv[b][:].rearrange("p (o h d) -> p o h d", o=1, h=H), name=f"v_out{b}")
        k.p.end_loop()


def experts(k):
    xh, xl = k.xh, k.xl
    with scope(k):
        gh, gl, uh, ul = (k.sb(n, [P, DC, NE * P], F32R) for n in ("gh", "gl", "uh", "ul"))
        dw = k.sb("dw", [P, NE, D])
        rw, rb, ln2 = k.sb("rw", [P, DC, 64]), k.sb("rb", [P, NR]), k.sb("ln2", [P, DC])
        with scope(k):
            g, u = k.sb("g", [P, DC, NE * P]), k.sb("u", [P, DC, NE * P])
            k.load((g[:], "moe_gate"), (u[:], "moe_up"), (dw[:], "moe_down"), (rw[:], "router_w"),
                   (rb[:], "router_b"), (ln2[:], "ln2_w"))
            mean, var = moments(k, k.h, "rms2")
            k.dve.tt(mean[:], mean[:], mean[:], ALU.mult, name="v")
            k.dve.wait("v")
            k.dve.tt(k.rms[:], mean[:], var[:], ALU.add, name="v")
            k.dve.wait("v")
            inverse_root(k, k.rms, "rms2")
            k.p.barrier()
            k.split(gh[:], gl[:], g[:], "g")
            k.split(uh[:], ul[:], u[:], "u")
        with scope(k):
            normalised_transpose(k, k.h, k.rms, ln2)
        probs, top = k.sb("probs", [P, NT, 8]), k.sb("top", [P, NT, 8])
        wts, picked = k.sb("wts", [P, NT, 8]), k.sb("picked", [P, NT, 8])
        idx, idxf = k.sb("idx", [P, NT, 8], U32), k.sb("idxf", [P, NT, 8])
        number = k.sb("number", [P, NT, 8])
        total = k.sb("total", [P, NT])
        v = k.dve
        with scope(k):
            pl = [k.ps("pl", [P, 64]) for _ in range(2)]
            xs = [k.sb("xs", [P, DC, P]) for _ in range(2)]
            v.memset(probs[:], -1.0, name="v")
            v.memset(number[:], 0.0, name="v")
            for e in range(1, NE):
                v.wait("v")
                v.memset(number[:, :, e], float(e), name="v")
            k.p.loop(NT // 2)
            for p in range(2):
                v.wait(f"l{p}")
                v.tt(xs[p][:], lambda i, p=p: f32(xh[:, :, ds((2 * i + p) * P, P)]),
                     lambda i, p=p: f32(xl[:, :, ds((2 * i + p) * P, P)]), ALU.add, name=f"xs{p}")
                k.pe.wait(f"xs{p}", f"lr{p}")
                k.pe.products(pl[p][:], [(xs[p][:, c, :], rw[:, c, :]) for c in range(DC)], name=f"l{p}")
                v.wait(f"l{p}")
                v.tt(lambda i, p=p: probs[:, ds(2 * i + p, 1), 0:NR], pl[p][:, 0:NR], rb[:], ALU.add, name=f"lr{p}")
            k.p.end_loop()
            lg = probs[:, :, 0:NR]
            k.act.act(lg, lg, ACT.Exp, scale=-1.0, name="sig")
            v.wait("sig")
            v.ts(lg, lg, 1.0, ALU.add, name="v")
            v.wait("v")
            v.recip(lg, lg, name="v")
            v.wait("v")
            for t in range(NT):
                v.op(lambda e, i, t=t: e.max(top[:, t, :], probs[:, t, :]), "v")
            v.wait("v")
            for t in range(NT):
                v.op(lambda e, i, t=t: e.max_index(idx[:, t, :], top[:, t, :], probs[:, t, :]), "v")
            v.wait("v")
            v.copy(idxf[:], idx[:], name="v")
            v.tt(total[:], top[:, :, 0], top[:, :, 1], ALU.add, name="v")
            v.wait("v")
            v.recip(total[:], total[:], name="v")
            v.wait("v")
            for s in range(2):
                v.tt(top[:, :, s], top[:, :, s], total[:], ALU.mult, name="v")
                v.tt(picked[:], number[:], idxf[:, :, s:s + 1].to_broadcast([P, NT, 8]), ALU.is_equal, name="v")
                v.wait("v")
                out = wts if s == 0 else picked
                v.tt(out[:], picked[:], top[:, :, s:s + 1].to_broadcast([P, NT, 8]), ALU.mult, name="v")
                v.wait("v")
            v.tt(wts[:], wts[:], picked[:], ALU.add, name="v")
            v.wait("v")
            v.ts(wts[:], wts[:], 0.125, ALU.mult, name="v")
            v.memset(total[:], 0.125, name="v")
        pg, pu = [k.ps("pg", [P, 512]) for _ in range(2)], [k.ps("pu", [P, 512]) for _ in range(2)]
        py = [k.ps("py", [P, D]) for _ in range(4)]
        sg = [k.sb("sg", [P, 512]) for _ in range(2)]
        hz = [k.sb("hz", [P, 512]) for _ in range(2)]
        k.p.loop(NB)
        for t in range(4):
            v.tt(lambda i, t=t: k.x[:, ds(4 * i + t, 1), :], lambda i, t=t: k.x[:, ds(4 * i + t, 1), :],
                 lambda i, t=t: k.h[:, ds(4 * i + t, 1), :], ALU.add, name=f"y_added{t}")
        behind = None

        def down(e, b):
            for t in range(4):
                k.pe.wait(f"fused{b}", f"y_read{t}")
                k.pe.mm(py[t][:], hz[b][:, t * P:(t + 1) * P], dw[:, e, :], name=f"y{t}")
                k.p.alias(f"down{b}", f"y{t}")
                v.wait(f"y{t}", f"y_added{t}")
                col = (lambda i, t=t: total[:, ds(4 * i + t, 1)]) if e == 0 else \
                    (lambda i, t=t, e=e: wts[:, ds(4 * i + t, 1), e - 1])
                v.stt(lambda i, t=t: k.x[:, ds(4 * i + t, 1), :], py[t][:], col,
                      lambda i, t=t: k.x[:, ds(4 * i + t, 1), :], ALU.mult, ALU.add, name=f"y_read{t}")
                k.p.alias(f"y_added{t}", f"y_read{t}")

        for e in range(NE):
            b = e % 2
            for wh, wl, out, n in ((gh, gl, pg[b], "g"), (uh, ul, pu[b], "u")):
                k.pe.wait(f"silu{b}" if n == "g" else f"fused{b}")
                k.pe.products(out[:], three(
                    lambda c: wh[:, c, e * P:(e + 1) * P], lambda c: wl[:, c, e * P:(e + 1) * P],
                    lambda c: lambda i, c=c: xh[:, c, ds(i * 512, 512)],
                    lambda c: lambda i, c=c: xl[:, c, ds(i * 512, 512)]), name=f"{n}{b}")
            k.act.wait(f"g{b}", f"fused{b}")
            k.act.act(sg[b][:], pg[b][:], ACT.Silu, name=f"silu{b}")
            v.wait(f"silu{b}", f"u{b}", f"down{b}")
            v.tt(hz[b][:], pu[b][:], sg[b][:], ALU.mult, name=f"fused{b}")
            if behind:
                down(*behind)
            behind = (e, b)
        down(*behind)
        k.p.end_loop()


def hopfield_weights(k):
    with scope(k):
        mem = k.sb("mem", [P, MC, P])
        wq, wk, wv, wo = k.sb("wq", [P, HH, D]), k.sb("wk", [P, HH, P]), k.sb("wv", [P, HH, P]), k.sb("wo", [P, HH, D])
        gm, bm, beta = k.sb("gm", [P, 1]), k.sb("bm", [P, 1]), k.sb("beta", [P, HH])
        k.load((mem[:], "memory"), (wq[:], "hop_q"), (wk[:], "hop_k"), (wv[:], "hop_v"), (wo[:], "hop_o"),
               (gm[:], "g_mem"), (bm[:], "b_mem"), (beta[:], "log_beta"))
        second_norm(k)
        k.act.act(beta[:], beta[:], ACT.Exp, name="beta")
        v, pe = k.dve, k.pe
        v.wait("beta")
        v.ts(beta[:], beta[:], 0.5, ALU.mult, name="v")
        mean, var = moments(k, mem, "mem", MC, P)
        inverse_root(k, var, "mem")
        mn, mt = k.sb("mn", [P, MC, P]), k.sb("mt", [P, NM])
        pt = k.ps("pt", [P, NM])
        for m in range(MC):
            v.ts(mn[:, m, :], mem[:, m, :], mean[:, m:m + 1], ALU.subtract, var[:, m:m + 1], ALU.mult, name="v")
        pe.wait("v")
        for m in range(MC):
            pe.transpose(pt[:, m * P:(m + 1) * P], mn[:, m, :], k.ident[:], name="mem_turned")
        v.wait("mem_turned")
        v.ts(mt[:], pt[:], gm[:], ALU.mult, bm[:], ALU.add, name="mt")
        kt, vt = [k.sb("kt", [P, NM]) for _ in range(2)], [k.sb("vt", [P, NM]) for _ in range(2)]
        pk, pv = k.ps("pk", [P, NM]), k.ps("pv", [P, NM])
        pa = [k.ps("pa", [P, 2, D]) for _ in range(3)]
        pe.wait("mt")
        for h in range(HH):
            b = h % 2
            pe.wait("kt0", "kt1", "vt0", "vt1")
            pe.mm(pk[:], wk[:, h, :], mt[:], name="k_in")
            pe.mm(pv[:], wv[:, h, :], mt[:], name="v_in")
            k.act.wait("k_in", f"c_in{b}")
            k.act.act(kt[b][:], pk[:], scale=beta[:, h:h + 1], name=f"kt{b}")
            v.wait("v_in", f"c_in{b}")
            v.copy(vt[b][:], pv[:], name=f"vt{b}")
            pe.wait(f"kt{b}", f"vt{b}", "a_out", "c_out")
            for n, (lhsT, rhs) in enumerate(((wq[:, h], kt[b]), (vt[b], kt[b]), (vt[b], wo[:, h]))):
                for m in range(2):
                    pe.mm(pa[n][:, m, :], lhsT[:, m * P:(m + 1) * P], rhs[:, :] if n < 2 else rhs,
                          name="c_in" + str(b) if n == 2 and m == 1 else None)
            k.act.wait(f"c_in{b}")
            v.wait(f"c_in{b}")
            k.act.act(k.to_scores[:, h], pa[0][:], name="a_out")
            k.act.act(k.again[:, h], pa[1][:], name="a_out")
            v.copy(k.to_out[:, h], pa[2][:], name="c_out")


def hopfield(k):
    with scope(k):
        gs, bs = k.sb("gs", [P, DC]), k.sb("bs", [P, DC])
        k.load((gs[:], "g_state"), (bs[:], "b_state"))
        k.p.barrier()
        pe, act, v, pool = k.pe, k.act, k.dve, k.pool
        xn = [k.sb("xn", [P, D]) for _ in range(2)]
        xt = [k.sb("xt", [P, DC, P]) for _ in range(2)]
        s = [k.sb("s", [P, HH, NM]) for _ in range(2)]
        r = [k.sb("r", [P, HH, NM]) for _ in range(2)]
        wt = [k.sb("wt", [P, MC, HH, P]) for _ in range(2)]
        cols = [k.sb("cols", [P, 8, HH]) for _ in range(2)]
        pss = [k.ps("pss", [P, 2, 2, NM]) for _ in range(2)]
        pt = [k.ps("pt", [P, 4, P]) for _ in range(2)]
        py = k.ps("py", [P, 512])
        pxt = k.ps("pxt", [P, DC, P])

        def state(p, u):
            v.wait(f"state{p}_in")
            v.ts(xn[p][:], lambda i: k.h[:, ds(u(i), 1), :], lambda i: k.hop_mean[:, ds(u(i), 1)],
                 ALU.subtract, lambda i: k.hop_scale[:, ds(u(i), 1)], ALU.mult, name=f"state{p}")
            pe.wait(f"state{p}", "state_out")
            for c in range(DC):
                pe.transpose(pxt[:, c, :], xn[p][:, c * P:(c + 1) * P], k.ident[:], name=f"state{p}_in")
            v.wait(f"state{p}_in", f"scores_a{p}")
            for c in range(DC):
                v.ts(xt[p][:, c, :], pxt[:, c, :], gs[:, c:c + 1], ALU.mult, bs[:, c:c + 1], ALU.add, name="state_out")

        def scores(p, step, q):
            rhs = k.again if step else k.to_scores
            half = q // 2
            pe.wait(f"weights{p}_{q}" if step else "state_out", f"s_out{half}")
            for h in range(2 * q, 2 * q + 2):
                for c in range(2):
                    lhsT = xt[p][:, c, :] if step == 0 else wt[p][:, c, h, :]
                    pe.mm(pss[half][:, q % 2, h % 2, :], lhsT, rhs[:, h, c, :], c == 0, c == 1,
                          name=f"scores{half}")
            k.p.alias(f"scores_a{p}", f"scores{half}")
            if q % 2:
                act.wait(f"scores{half}", f"s_read{p}")
                act.act(s[p][:, 4 * half:4 * half + 4, :],
                        pss[half][:].rearrange("p a b n -> p (a b) n"), name=f"s_out{half}")
                k.p.alias(f"s{p}", f"s_out{half}")

        def largest(p, half):
            v.wait(f"s{p}", f"tau_read{p}")
            v.reduce(cols[p][:, 0, 4 * half:4 * half + 4], s[p][:, 4 * half:4 * half + 4, :], ALU.max, name=f"t{p}")

        def start(p):
            tau = cols[p][:, 0, :]
            largest(p, 1)
            v.wait(f"t{p}")
            v.ts(tau, tau, -1.0, ALU.add, name=f"t{p}")

        def sums(p, g):
            tau, neg, sq, root, total, slope = (cols[p][:, n, :] for n in range(6))
            if g == 0:
                v.wait(f"t{p}", f"sq{p}")
                v.ts(neg, tau, -1.0, ALU.mult, name=f"neg{p}")
                v.wait(f"r_turned{p}")
            for h in range(2 * g, 2 * g + 2):
                v.ts(r[p][:, h, :], s[p][:, h, :], tau[:, h:h + 1], ALU.max, 0.0, ALU.add,
                     accum=total[:, h:h + 1], name=f"r{p}")
                act.wait(f"r{p}", f"neg{p}", f"newton{p}")
                act.act(r[p][:, h, :], r[p][:, h, :], ACT.Square, bias=neg[:, h:h + 1],
                        accum=sq[:, h:h + 1], name=f"sq{p}")
            if g == 3:
                act.wait(f"sq{p}")
                act.act(root, sq, ACT.Sqrt, name=f"root{p}")

        def newton(p):
            tau, neg, sq, root, total, slope = (cols[p][:, n, :] for n in range(6))
            v.wait(f"r{p}")
            v.stt(slope, tau, -float(NM), total, ALU.mult, ALU.add, name=f"slope{p}")
            v.wait(f"slope{p}")
            v.recip(slope, slope, name=f"slope{p}")
            v.wait(f"root{p}")
            v.tt(root, sq, root, ALU.subtract, name=f"newton{p}")
            v.wait(f"newton{p}", f"slope{p}")
            v.tt(root, root, slope, ALU.mult, name=f"newton{p}")
            v.wait(f"newton{p}")
            v.tt(tau, tau, root, ALU.add, name=f"t{p}")

        def above(p, g):
            tau = cols[p][:, 0, :]
            v.wait(f"t{p}", f"sq{p}")
            for h in range(2 * g, 2 * g + 2):
                v.ts(r[p][:, h, :], s[p][:, h, :], tau[:, h:h + 1], ALU.subtract, 0.0, ALU.max, name=f"r{p}_{h}")
            k.p.alias(f"s_read{p}", f"r{p}_{2 * g + 1}")
            k.p.alias(f"tau_read{p}", f"r{p}_{2 * g + 1}")

        def weights(p, g):
            b = g % 2
            pe.wait(f"r{p}_{2 * g + 1}", f"w_out{b}")
            for c in range(2):
                for h in range(2):
                    pe.transpose(pt[b][:, 2 * c + h, :], r[p][:, 2 * g + h, c * P:(c + 1) * P], k.ident[:],
                                 name=f"turned{b}")
            k.p.alias(f"r_turned{p}", f"turned{b}")
            act.wait(f"turned{b}", f"scores_a{p}", f"y_in{p}")
            act.act(wt[p][:, :, 2 * g:2 * g + 2, :], pt[b][:].rearrange("p (c h) t -> p c h t", c=2),
                    ACT.Square, name=f"w_out{b}")
            k.p.alias(f"weights{p}_{g}", f"w_out{b}")

        def result(p, u, q):
            pe.wait(f"weights{p}_{q}", "y_out")
            for h in range(2 * q, 2 * q + 2):
                for c in range(2):
                    end = (h, c) == (HH - 1, 1)
                    pe.mm(py[:, 0:D], wt[p][:, c, h, :], k.to_out[:, h, c, :], (h, c) == (0, 0), end,
                          name=f"y_in{p}" if end else None)
            if q == 3:
                v.wait(f"y_in{p}")
                v.tt(lambda i: k.x[:, ds(u(i), 1), :], lambda i: k.x[:, ds(u(i), 1), :], py[:, 0:D],
                     ALU.add, name="y_out")

        def chain(p, first, last):
            out = [("products", [[(state, p, first)], [], [(scores, p, 0, 0)], []]),
                   ("products", [[(scores, p, 0, 1)], [(scores, p, 0, 2)], [], [(largest, p, 0)],
                                [(scores, p, 0, 3)]])]

            def slot(kind, before, f):
                out.append((kind, [[before, (f, p, 0)]] + [[(f, p, g)] for g in range(1, 4)]))
            for step in range(3):
                slot("start", (start, p), sums)
                for _ in range(NEWTON - 1):
                    slot("sums", (newton, p), sums)
                slot("above", (newton, p), above)
                then = (lambda q, n=step + 1: scores(p, n, q)) if step < 2 else (lambda q: result(p, last, q))
                out.append(("products", [[(weights, p, 0)], [(weights, p, 1)], [(weights, p, 2), (then, 0)],
                                         [(weights, p, 3)]]))
                out.append(("products", [[(then, 1)], [(then, 2)], [], [(largest, p, 0)] if step < 2 else [],
                                         [(then, 3)]]))
            return out

        def together(*slots):
            slots = sorted(slots, key=lambda s: ("products", "sums", "start", "above").index(s[0]))
            if [kind for kind, _ in slots] in (["sums", "sums"], ["sums", "start"]):
                units = [u for _, us in slots for u in us]
            else:
                units = [us[n] for n in range(5) for _, us in slots if n < len(us)]
            for unit in units:
                for f, *a in unit:
                    f(*a)

        even = chain(0, lambda i: 2 * i, lambda i: 2 * i)
        cut = len(even) // 2
        for part in chain(1, lambda i: NT - 1, None)[:cut]:
            together(part)
        k.p.loop(NT // 2)
        odd = chain(1, lambda i: 2 * i + 1, lambda i: (2 * i + NT - 1) % NT)
        for a, b in zip(even, odd[cut:] + odd[:cut]):
            together(a, b)
        k.p.end_loop()


def two_layer_kernel(nc, ins, out, only=None):
    with ExitStack() as ctx:
        k = Kernel(nc, ctx, ins, out)
        k.rec_q = nc.dram_tensor("rec_q", [B * H, REC, S], F32, kind="Internal").ap()
        k.rec_k = nc.dram_tensor("rec_k", [B * H, REC, S], F32, kind="Internal").ap()
        k.x = k.sb("x", [P, NT, D])
        constants(k)
        blend = k.sb("blend", [P, 2, 4, 2])
        k.p.barrier()
        with scope(k):
            k.vals = k.sb("vals", [P, NT, H, 32])
            k.heads = k.sb("heads", [P, B * H, QT, HD])
            with scope(k):
                k.xh, k.xl = k.sb("xh", [P, DC, T], F32R), k.sb("xl", [P, DC, T], F32R)
                first_norm(k)
                blend_weights(k, blend)
                queries_and_keys(k)
                swiglu(k)
            attention(k, ["gsa", "std"], [blend[:, 0], blend[:, 1]])
            output_projection(k, "wo0", k.x)
        k.h = k.sb("h", [P, NT, D])
        k.hop_mean, k.hop_scale, k.rms = k.sb("hop_mean", [P, NT]), k.sb("hop_scale", [P, NT]), k.sb("rms", [P, NT])
        with scope(k):
            k.to_scores, k.again, k.to_out = (k.sb(n, [P, HH, 2, NM]) for n in ("to_scores", "again", "to_out"))
            hopfield_weights(k)
            hopfield(k)
        with scope(k):
            k.vals = k.sb("vals", [P, NT, H, 32])
            k.heads = k.sb("heads", [P, B * H, QT, HD])
            with scope(k):
                k.xh, k.xl = k.sb("xh", [P, DC, T], F32R), k.sb("xl", [P, DC, T], F32R)
                latent_projections(k)
            one = k.sb("one", [P, 4, 2])
            k.pool.memset(one[:], 1.0, name="one")
            k.pool.wait("one")
            attention(k, ["std"], [one[:]])
            output_projection(k, "lat_o", k.h)
        with scope(k):
            k.xh, k.xl = k.sb("xh", [P, DC, T], F32R), k.sb("xl", [P, DC, T], F32R)
            experts(k)
        k.sp.dma(out, k.x[:], k.dma_counter("result"), "result")
        k.p.barrier()
        block = ctx.enter_context(nc.Block())
        block.sync(lambda e: k.sp.play(e))
        block.scalar(lambda e: k.act.play(e))
        block.vector(lambda e: k.dve.play(e))
        block.gpsimd(lambda e: k.pool.play(e))
        block.tensor(lambda e: k.pe.play(e))


def blend_weights(k, blend):
    with scope(k):
        sc, b = k.sb("sc", [P, 5]), k.sb("b", [P, 2])
        k.load((sc[:], "splat_scalars"))
        k.p.barrier()
        v = k.dve
        k.act.act(b[:, 0:1], sc[:, 4:5], ACT.Exp, scale=-1.0, name="b")
        v.wait("b")
        for op, s1, o2, s2 in ((ALU.add, 1.0, None, None), (None,) * 4, (ALU.mult, 0.15, ALU.min, 0.03)):
            if op is None:
                v.recip(b[:, 0:1], b[:, 0:1], name="v")
            elif o2 is None:
                v.ts(b[:, 0:1], b[:, 0:1], s1, op, name="v")
            else:
                v.ts(b[:, 0:1], b[:, 0:1], s1, op, s2, o2, name="v")
            v.wait("v")
        v.ts(b[:, 1:2], b[:, 0:1], -1.0, ALU.mult, 1.0, ALU.add, name="v")
        v.wait("v")
        for n in range(2):
            v.copy(blend[:, n], b[:, n:n + 1].unsqueeze(2).to_broadcast([P, 4, 2]), name="v")




def layout(a):
    f = {n: np.asarray(v, np.float32) if np.ndim(v) == 0 else np.asarray(v) for n, v in a.items()}

    def rows(w):
        return w.reshape(-1, P, w.shape[1]).transpose(1, 0, 2)

    def spread(v, n=P):
        return np.broadcast_to(np.asarray(v).reshape(1, -1), (n, np.asarray(v).size))

    def col(v):
        return v.reshape(-1, P).T

    o = {}
    x = rows(f["L0_attn_hidden_states"].reshape(T, D))
    o["x_a"], o["x_b"] = x[:, :NT // 2], x[:, NT // 2:]
    o["wqk0"] = rows(np.concatenate([f["L0_attn_Wq"].T, f["L0_attn_Wk"].T], 1))
    o["wv0"], o["wo0"] = rows(f["L0_attn_Wv"].T), rows(f["L0_attn_Wo"].T)
    pos, dirs = f["L0_attn_splat_positions"], f["L0_attn_splat_directions"]
    for name, t in (("splat_pos", pos), ("splat_dir", dirs), ("neg_half", None)):
        m = np.zeros((D, H * NS), np.float32)
        for h in range(H):
            m[h * HD:(h + 1) * HD, h * NS:(h + 1) * NS] = -0.5 if t is None else t[h].T
        o[name] = rows(m)
    o["pos_rows"], o["dir_rows"] = pos.reshape(P, HD), dirs.reshape(P, HD)
    o["splat_scalars"] = np.concatenate(
        [f["L0_attn_splat_log_scales"].reshape(P, 1), f["L0_attn_splat_log_amplitudes"].reshape(P, 1)]
        + [spread(f["L0_attn_" + n]) for n in ("directional_strength", "position_sensitivity", "gsa_strength")], 1)
    o["gate_w"], o["up_w"], o["down_w"] = (rows(f[f"L0_ffn_{n}_w"]).reshape(P, -1) for n in ("gate", "up", "down"))
    o["gate_s"], o["up_s"] = col(f["L0_ffn_gate_scale"]), col(f["L0_ffn_up_scale"])
    o["down_s"] = spread(f["L0_ffn_down_scale"])
    o["memory"] = rows(f["L1_attn_memory"])
    o["hop_q"] = rows(f["L1_attn_Wq"])
    for n, w in (("hop_k", "Wk"), ("hop_v", "Wv")):
        o[n] = f["L1_attn_" + w].T.reshape(P, HH, P)
    o["hop_o"] = rows(f["L1_attn_Wo"].T)
    o["g_mem"], o["b_mem"] = col(f["L1_attn_g_mem"]), col(f["L1_attn_b_mem"])
    o["g_state"], o["b_state"] = col(f["L1_attn_g_state"]), col(f["L1_attn_b_state"])
    o["log_beta"] = spread(f["L1_attn_log_beta"])
    g = {n[7:]: v for n, v in f.items() if n.startswith("L1_ffn_")}
    R, LAT = HD // 2, D // 4
    o["ln1_w"], o["ln2_w"] = col(g["ln1_w"]), col(g["ln2_w"])
    o["lat_down"] = rows(np.concatenate([g["kv_d_w"], g["q_d_w"]], 1))

    def heads(w, plain):
        m = np.zeros((w.shape[0], H, HD), np.float32)
        m[:, :, (0 if plain else R):(R if plain else HD)] = w.reshape(-1, H, R)
        return m.reshape(-1, D)

    def swapped(w):
        return w.reshape(-1, H, 2, R // 2)[:, :, ::-1].reshape(-1, H * R)

    qa = np.zeros((w := P, H, HD), np.float32)
    qa[LAT:, :, :R], qa[LAT:, :, R:] = g["q_u_w"].reshape(-1, H, R), g["rope_q_w"].reshape(-1, H, R)
    o["lat_qa"] = qa.reshape(P, D)
    o["lat_qb"] = np.concatenate([np.zeros((LAT, D), np.float32), heads(swapped(g["rope_q_w"]), False)])
    o["lat_kd"] = np.concatenate([heads(g["k_u_w"], True), np.zeros((LAT, D), np.float32)])
    o["lat_ka"], o["lat_kb"] = rows(heads(g["rope_k_w"], False)), rows(heads(swapped(g["rope_k_w"]), False))
    o["lat_v"] = np.concatenate([g["v_u_w"], np.zeros((LAT, D), np.float32)])
    o["lat_o"] = rows(g["o_w"])
    freq = (1.0 / np.float32(10000.0) ** (np.arange(0, R, 2, dtype=np.float32) / np.float32(R))).astype(np.float32)
    ang = np.outer(np.arange(S, dtype=np.float32), freq).astype(np.float32)
    ang = np.concatenate([ang, ang], 1)
    cos, sin = np.ones((HD, S), np.float32), np.zeros((HD, S), np.float32)
    cos[R:] = np.cos(ang).T
    sin[R:] = np.sin(ang).T
    sin[R:R + R // 2] *= -1
    o["rope_cos"], o["rope_sin"] = np.tile(cos, (8, B)), np.tile(sin, (8, B))
    for n in ("gate", "up"):
        w = np.concatenate([g["sh_" + n][None], g["r_" + n]])
        o["moe_" + n] = w.reshape(NE, DC, P, P).transpose(2, 1, 0, 3).reshape(P, DC, NE * P)
    o["moe_down"] = np.concatenate([g["sh_down"][None], g["r_down"]]).transpose(1, 0, 2)
    o["router_w"] = rows(np.concatenate([g["router_w"], np.zeros((D, 64 - NR), np.float32)], 1))
    o["router_b"] = spread(g["router_b"])
    return {n: np.ascontiguousarray(v) for n, v in o.items()}


def kernel(**inputs):
    import concourse.bacc as bacc
    from concourse.bass_utils import run_bass_kernel_spmd

    nc = bacc.Bacc("TRN2", target_bir_lowering=False, num_devices=1)
    arrays = layout(inputs)
    ins = {n: nc.dram_tensor("in_" + n, a.shape, mybir.dt.from_np(a.dtype), kind="ExternalInput").ap()
           for n, a in arrays.items()}
    out = nc.dram_tensor("out", (P, NT, D), F32, kind="ExternalOutput").ap()
    two_layer_kernel(nc, ins, out)
    r = run_bass_kernel_spmd(nc, [{"in_" + n: a for n, a in arrays.items()}], core_ids=[0])
    return np.ascontiguousarray(r.results[0]["out"].transpose(1, 0, 2).reshape(B, S, D))
```
